# Optimizing a Trainium2 kernel written in Bass

```python
import numpy as np
import jax
import jax.numpy as jnp

def _softmax(x, axis=-1):
    return jax.nn.softmax(x, axis=axis)

def _gelu(x):
    return jax.nn.gelu(x, approximate=True)

def _silu(x):
    return jax.nn.silu(x)

def _sigmoid(x):
    return jax.nn.sigmoid(x)

def _layernorm(x, axis=-1, eps=1e-05):
    m = jnp.mean(x, axis=axis, keepdims=True)
    v = jnp.var(x, axis=axis, keepdims=True)
    return (x - m) / jnp.sqrt(v + eps)

def _scatter_add(tgt, idx, src, axis=0):
    return tgt.at[idx].add(src)

def _segment_sum(src, seg, n):
    return jax.ops.segment_sum(src, seg, n)
kernel_name = 'mk_gnn_resnorm_d1_gnn_r32_a27dbc'

def setup_inputs(seed: int=0):
    np.random.seed(seed)
    _w = jnp.asarray

    def _rec_inputs():
        import jax
        import jax.numpy as jnp
        _gk = jax.random.key(seed)
        x = -0.000202 + 1 * jax.random.normal(jax.random.fold_in(_gk, 1), (25000, 256), jnp.float32)
        src = jax.random.randint(jax.random.fold_in(_gk, 2), (12500,), 0, 25000, jnp.int32)
        dst = jax.random.randint(jax.random.fold_in(_gk, 3), (12500,), 0, 25000, jnp.int32)
        _o = jnp.argsort(dst, stable=True)
        src = src[_o]
        dst = dst[_o]
        edge_attr_256 = -5.16925e-05 + 1.00005 * jax.random.normal(jax.random.fold_in(_gk, 11), (12500, 256), jnp.float32)
        return (x, src, dst, edge_attr_256)
    x, src, dst, edge_attr_256 = _rec_inputs()

    def _L0_gnn_setup():
        import jax, jax.numpy as jnp
        import numpy as np
        N, E, F = (25000, 12500, 256)
        EPS = 1e-05

        def _bn(h, gamma, beta):
            mu = jnp.mean(h, axis=0)
            var = jnp.var(h, axis=0)
            return (h - mu) * jax.lax.rsqrt(var + EPS) * gamma + beta
        key = jax.random.key(seed)
        ks = jax.random.split(key, 8)

        def w(k, shape):
            return jax.random.normal(k, shape, jnp.float32) * 0.05
        return {'x': jax.random.normal(ks[0], (N, F), jnp.float32), 'edge_index': jax.random.randint(ks[1], (2, E), 0, N, dtype=jnp.int32), 'edge_attr': jax.random.normal(ks[2], (E, F), jnp.float32), 'w_full1': w(ks[3], (F, 3 * F)), 'b_full1': jnp.zeros((F,), jnp.float32), 'w_full2': w(ks[4], (F, F)), 'b_full2': jnp.zeros((F,), jnp.float32), 'w_n1': w(ks[5], (F, 3 * F)), 'b_n1': jnp.zeros((F,), jnp.float32), 'w_n2': w(ks[6], (F, F)), 'b_n2': jnp.zeros((F,), jnp.float32), 'gamma_int': jnp.ones((F,), jnp.float32), 'beta_int': jnp.zeros((F,), jnp.float32), 'gamma_bn': jnp.ones((F,), jnp.float32), 'beta_bn': jnp.zeros((F,), jnp.float32)}
    _L0_gnn_all = _L0_gnn_setup()
    _L0_gnn_in = {k: v for k, v in _L0_gnn_all.items() if k in ('w_full1', 'b_full1', 'w_full2', 'b_full2', 'w_n1', 'b_n1', 'w_n2', 'b_n2', 'gamma_int', 'beta_int', 'gamma_bn', 'beta_bn')}
    del _L0_gnn_all
    return {'x': x, 'src': src, 'dst': dst, 'edge_attr_256': edge_attr_256, 'L0_gnn_w_full1': _L0_gnn_in['w_full1'], 'L0_gnn_b_full1': _L0_gnn_in['b_full1'], 'L0_gnn_w_full2': _L0_gnn_in['w_full2'], 'L0_gnn_b_full2': _L0_gnn_in['b_full2'], 'L0_gnn_w_n1': _L0_gnn_in['w_n1'], 'L0_gnn_b_n1': _L0_gnn_in['b_n1'], 'L0_gnn_w_n2': _L0_gnn_in['w_n2'], 'L0_gnn_b_n2': _L0_gnn_in['b_n2'], 'L0_gnn_gamma_int': _L0_gnn_in['gamma_int'], 'L0_gnn_beta_int': _L0_gnn_in['beta_int'], 'L0_gnn_gamma_bn': _L0_gnn_in['gamma_bn'], 'L0_gnn_beta_bn': _L0_gnn_in['beta_bn']}

def reference(x, src, dst, edge_attr_256, L0_gnn_w_full1, L0_gnn_b_full1, L0_gnn_w_full2, L0_gnn_b_full2, L0_gnn_w_n1, L0_gnn_b_n1, L0_gnn_w_n2, L0_gnn_b_n2, L0_gnn_gamma_int, L0_gnn_beta_int, L0_gnn_gamma_bn, L0_gnn_beta_bn):
    import jax
    import jax.numpy as jnp

    def _L0_gnn_ref(x, edge_index, edge_attr, w_full1, b_full1, w_full2, b_full2, w_n1, b_n1, w_n2, b_n2, gamma_int, beta_int, gamma_bn, beta_bn):
        import jax, jax.numpy as jnp
        import numpy as np
        N, E, F = (25000, 12500, 256)
        EPS = 1e-05

        def _bn(h, gamma, beta):
            mu = jnp.mean(h, axis=0)
            var = jnp.var(h, axis=0)
            return (h - mu) * jax.lax.rsqrt(var + EPS) * gamma + beta
        src = edge_index[0]
        dst = edge_index[1]
        feat = jnp.concatenate([x[dst], x[src], edge_attr], axis=1)
        h = jax.nn.silu(feat @ w_full1.T + b_full1) @ w_full2.T + b_full2
        score = jax.nn.sigmoid(_bn(h, gamma_int, beta_int))
        m = jax.nn.silu(feat @ w_n1.T + b_n1) @ w_n2.T + b_n2
        msg = score * m
        out = jax.ops.segment_sum(msg, dst, num_segments=N)
        return jax.nn.relu(x + _bn(out, gamma_bn, beta_bn))
    edge_index = jnp.stack([src, dst])
    x = _layernorm(x + _L0_gnn_ref(x, edge_index, edge_attr_256, L0_gnn_w_full1, L0_gnn_b_full1, L0_gnn_w_full2, L0_gnn_b_full2, L0_gnn_w_n1, L0_gnn_b_n1, L0_gnn_w_n2, L0_gnn_b_n2, L0_gnn_gamma_int, L0_gnn_beta_int, L0_gnn_gamma_bn, L0_gnn_beta_bn), axis=-1)
    return x

_drawn_inputs = setup_inputs


def setup_inputs(seed=0):
    import zlib

    import numpy as np

    out = dict(_drawn_inputs(seed))
    spreads = {'L0_gnn_b_full1': (0.0, 0.8),
     'L0_gnn_b_full2': (0.0, 0.8),
     'L0_gnn_b_n1': (0.0, 0.295),
     'L0_gnn_b_n2': (0.0, 0.1),
     'L0_gnn_gamma_int': (1.0, 0.6),
     'L0_gnn_beta_int': (0.0, 0.8),
     'L0_gnn_gamma_bn': (1.0, 0.2),
     'L0_gnn_beta_bn': (0.0, 0.1)}
    factors = {}
    for name, (base, spread) in spreads.items():
        noise = np.random.default_rng([zlib.crc32(name.encode()), seed]).standard_normal(out[name].shape)
        drawn = base * np.exp(spread * noise) if base else spread * noise
        out[name] = jnp.asarray(drawn.astype(out[name].dtype))
    for name, factor in factors.items():
        out[name] = (out[name] * factor).astype(out[name].dtype)
    return out
```

```python
from contextlib import ExitStack

import concourse.bass as bass
from concourse import mybir

F32 = mybir.dt.float32
F32R = mybir.dt.float32r
I32 = mybir.dt.int32
ALU = mybir.AluOpType
ACT = mybir.ActivationFunctionType

P = 128
EPS = 1e-5


def in_order(eng, body, pieces, ring):
    for first, count in pieces:
        looped = count // ring * ring if count >= 2 * ring else 0
        if looped:
            with eng.Fori(0, looped // ring) as i:
                for u in range(ring):
                    s = first + u
                    body(i * ring + s, s % ring, i + s // ring)
        for s in range(first + looped, first + count):
            body(s, s % ring, s // ring)


def gnn_program(nc, x, src, dst, edge_attr, w_full1, b_full1, w_full2, b_full2,
                w_n1, b_n1, w_n2, b_n2, gamma_int, beta_int, gamma_bn, beta_bn, out):
    N, F = x.shape
    E = edge_attr.shape[0]
    KC = 3 * F // P
    MC = F // P
    TG = 4
    GE = TG * P
    G = E // GE
    REST = E - G * GE
    TAIL = [min(P, REST - t * P) for t in range((REST + P - 1) // P)]
    assert 0 < REST and len(TAIL) == 2
    NT = (E + P - 1) // P
    DUMP = GE
    TR = (N + DUMP + 1023) // 1024 * 1024
    ZR = TR // (G + 1) // P
    assert ZR * P * (G + 1) == TR

    RJ = 5
    NJ = N // P
    C = NJ // RJ
    assert C * RJ == NJ
    NTAIL = N - NJ * P
    NMAIN = NJ * P
    RES = 24

    hm_dram = nc.dram_tensor("hm_dram", (G + 1, P, TG * 2 * F), F32, kind="Internal").ap()
    table = nc.dram_tensor("node_table", (TR, F), F32, kind="Internal").ap()

    w1 = [w_full1, w_n1]
    w2 = [w_full2, w_n2]
    b1 = [b_full1, b_n1]
    b2 = [b_full2, b_n2]
    H, M = 0, 1

    ctx = ExitStack()

    def sem(name):
        return ctx.enter_context(nc.semaphore(name))

    def rows_of(g):
        return [P] * TG if not (isinstance(g, int) and g == G) else TAIL

    with ctx:
        def keep(name, shape, dt=F32):
            return ctx.enter_context(nc.sbuf_tensor(name, shape, dt))

        bank = ctx.enter_context(nc.psum_tensor("bank", [P, 8, 512], F32))
        ident = keep("ident", [P, P])
        ones = keep("ones", [P, P])
        dst_col = keep("dst_col", [P, (G + 1) * TG])
        scatter_idx = keep("scatter_idx", [P, (G + 1) * TG], I32)
        earlier = keep("earlier", [P, (G + 1) * TG])
        gam = keep("gam", [P, 2, F])
        bet = keep("bet", [P, 2, F])
        A = keep("A", [P, 2, F])
        Bc = keep("Bc", [P, 2, F])
        bn_t = keep("bn_t", [P, 4, F])

        passed = {n: sem("passed_" + n) for n in ("sp", "act", "pool")}

        def pass_waits(eng, n):
            eng.sem_inc(passed[n], 1)

        def bn_coefficients(dve, which, sums, squares, count, step, var_done, std_done):
            mean, ex2, var, rstd = (bn_t[:, i, :] for i in range(4))
            n = [0]

            def link(ins):
                n[0] += 1
                ins.then_inc(step, 1)
                dve.wait_ge(step, n[0])
            link(dve.tensor_scalar(mean, sums, 1.0 / count, None, ALU.mult))
            link(dve.tensor_scalar(ex2, squares, 1.0 / count, None, ALU.mult))
            link(dve.tensor_tensor(var, mean, mean, ALU.mult))
            link(dve.tensor_tensor(var, ex2, var, ALU.subtract))
            dve.tensor_scalar(var, var, 0.0, EPS, ALU.max, ALU.add).then_inc(var_done, 1)
            dve.wait_ge(std_done, 1)
            link(dve.reciprocal(rstd, var))
            link(dve.tensor_tensor(A[:, which, :], rstd, gam[:, which, :], ALU.mult))
            link(dve.tensor_tensor(ex2, mean, A[:, which, :], ALU.mult))
            link(dve.tensor_tensor(Bc[:, which, :], bet[:, which, :], ex2, ALU.subtract))

        def bn_std(act, var_done, std_done):
            act.wait_ge(var_done, 1)
            act.activation(bn_t[:, 2, :], bn_t[:, 2, :], ACT.Sqrt).then_inc(std_done, 1)

        with ExitStack() as s1:
            def sb(name, shape, dt=F32):
                return s1.enter_context(nc.sbuf_tensor(name, shape, dt))
            w1hl = [sb("w1_hi", [P, 2, KC, F], F32R), sb("w1_lo", [P, 2, KC, F], F32R)]
            w2hl = [sb("w2_hi", [P, 2, MC, F], F32R), sb("w2_lo", [P, 2, MC, F], F32R)]
            xT = [sb("xT_hi", [P, KC, GE], F32R), sb("xT_lo", [P, KC, GE], F32R)]
            g_hl = [sb("g_hi", [P, 2, MC, GE], F32R), sb("g_lo", [P, 2, MC, GE], F32R)]
            w1_raw = sb("w1_raw", [P, 2, MC, 3 * F])
            w2_raw = sb("w2_raw", [P, 2, MC, F])
            land = sb("land", [P, 2, 3, TG, F])
            g32 = sb("g32", [P, 2, GE])
            hm = sb("hm", [P, 2, TG, 2 * F])
            hsq = sb("hsq", [P, TG, F])
            acc = sb("acc", [P, 2, TG, F])
            b1c = sb("b1c", [P, 2, MC])
            b2b = sb("b2b", [P, 2, F])
            drow = sb("drow", [P, 2, GE], I32)
            before = sb("before", [P, GE])
            scratch = sb("scratch", [P, 10 * P])
            zero = sb("zero", [P, F])
            idx_raw = sb("idx_raw", [P, 2, P], I32)
            idx_f = sb("idx_f", [P, 2, P])
            idx = sb("idx", [P, 2, (G + 1) * TG], I32)
            cur = sb("cur", [P, 2, 2, TG], I32)
            lane = sb("lane", [P, G + 1, TG], I32)
            lane_f = sb("lane_f", [P, (G + 1) * TG])
            dup = sb("dup", [P, (G + 1) * TG])

            c_ident, c_ones, c_mask = sem("c_ident"), sem("c_ones"), sem("c_mask")
            c_zero, c_acc, c_idx = sem("c_zero"), sem("c_acc"), sem("c_idx")
            idx_in, w_in, vec_in = sem("idx_in"), sem("w_in"), sem("vec_in")
            idx_float, idx_turned, idx_ready = sem("idx_float"), sem("idx_turned"), sem("idx_ready")
            w_turned, w_hi, w_lo = sem("w_turned"), sem("w_hi"), sem("w_lo")
            cur_ready = sem("cur_ready")
            land_x = [sem("land_x0"), sem("land_x1")]
            land_e = [sem("land_e0"), sem("land_e1")]
            drow_in = [sem("drow_in0"), sem("drow_in1")]
            turned, hi_ready, lo_ready = sem("turned"), sem("hi_ready"), sem("lo_ready")
            l1h_done, l1n_step = sem("l1h_done"), sem("l1n_step")
            silu_done, ghi_ready, glo_ready = sem("silu_done"), sem("ghi_ready"), sem("glo_ready")
            l2_done = [sem("l2h_done"), sem("l2n_done")]
            taken = [sem("h_taken"), sem("m_taken")]
            squared, summed = sem("squared"), sem("summed")
            stored = [sem("hm_stored0"), sem("hm_stored1")]
            counted, zeroed = sem("counted"), sem("zeroed")
            stats_done, bn1, idx_step = sem("stats_done"), sem("bn1"), sem("idx_step")
            bn1_var, bn1_std = sem("bn1_var"), sem("bn1_std")
            lane_made = sem("lane_made")

            bank_of = [[0, 1], [2, 3]]
            TURN, L2 = 4, 6
            units = [(1, b, k) for b in range(2) for k in range(KC)] + \
                    [(2, b, k) for b in range(2) for k in range(MC)]

            def edge_rows(g, t0, rows):
                return edge_attr[bass.ds(g * GE + t0 * P, rows), :]

            block = s1.enter_context(nc.Block())

            @block.sync
            def _(sp):
                sp.wait_ge(c_idx, 1)
                last = (NT - 1) * P
                for i, v in enumerate((dst, src)):
                    sp.dma_start(idx_raw[0:NT - 1, i, :], v[0:last].rearrange("(t p) -> t p", p=P)).then_inc(idx_in, 16)
                    sp.dma_start(idx_raw[NT - 1:NT, i, 0:E - last],
                                 v[last:E].rearrange("(o p) -> o p", o=1)).then_inc(idx_in, 16)

                def load_rows(g, slot):
                    rows = rows_of(g)
                    if len(rows) == TG:
                        sp.dma_start(land[:, slot, 2, :, :],
                                     edge_rows(g, 0, GE).rearrange("(t p) f -> p t f", p=P)).then_inc(land_e[slot], 16)
                        sp.dma_start(drow[:, slot, :], dst[bass.ds(g * GE, GE)].rearrange("(o n) -> o n", o=1)
                                     .to_broadcast([P, GE])).then_inc(drow_in[slot], 16)
                    else:
                        for t, r in enumerate(rows):
                            sp.dma_start(land[0:r, slot, 2, t, :], edge_rows(g, t, r)).then_inc(land_e[slot], 16)
                        sp.dma_start(drow[:, slot, 0:REST], dst[G * GE:E].rearrange("(o n) -> o n", o=1)
                                     .to_broadcast([P, REST])).then_inc(drow_in[slot], 16)

                for b in range(2):
                    sp.dma_start(w1_raw[:, b, :, :], w1[b].rearrange("(c m) k -> m c k", m=P)).then_inc(w_in, 16)
                load_rows(0, 0)
                for b in range(2):
                    sp.dma_start(w2_raw[:, b, :, :], w2[b].rearrange("(c m) k -> m c k", m=P)).then_inc(w_in, 16)
                    sp.dma_start(b1c[:, b, :], b1[b].rearrange("(c m) -> m c", m=P), allow_slow_non_contiguous=True).then_inc(vec_in, 16)
                    sp.dma_start(b2b[:, b, :], b2[b].rearrange("(o f) -> o f", o=1).to_broadcast([P, F])).then_inc(vec_in, 16)
                for i, (gv, bv) in enumerate(((gamma_int, beta_int), (gamma_bn, beta_bn))):
                    sp.dma_start(gam[:, i, :], gv.rearrange("(o f) -> o f", o=1).to_broadcast([P, F])).then_inc(vec_in, 16)
                    sp.dma_start(bet[:, i, :], bv.rearrange("(o f) -> o f", o=1).to_broadcast([P, F])).then_inc(vec_in, 16)
                load_rows(1, 1)
                sp.wait_ge(c_zero, 1)

                def store(g, slot):
                    sp.wait_ge(taken[H], g * 2 + 2)
                    pass_waits(sp, "sp")
                    sp.wait_ge(taken[M], g * 2 + 2)
                    pass_waits(sp, "sp")
                    sp.dma_start(hm_dram[bass.ds(g, 1), :, :].rearrange("o p n -> (o p) n"),
                                 hm[:, slot, :, :].rearrange("p t n -> p (t n)")).then_inc(stored[slot], 16)

                def body(g, slot, turn):
                    sp.dma_start(table[bass.ds(g * (P * ZR), P * ZR), :].rearrange("(p j) f -> p j f", p=P),
                                 zero[:, :].unsqueeze(1).to_broadcast([P, ZR, F])).then_inc(zeroed, 16)
                    if not (isinstance(g, int) and g == 0):
                        store(g - 1, 1 - slot)
                    if not (isinstance(g, int) and g + 2 > G):
                        sp.wait_ge(turned, KC * g + KC)
                        pass_waits(sp, "sp")
                        sp.wait_ge(counted, g + 1)
                        pass_waits(sp, "sp")
                        load_rows(g + 2, slot)

                in_order(sp, body, [(0, 1), (1, G - 4), (G - 3, 1), (G - 2, 3)], 2)
                sp.wait_ge(taken[M], 2 * G + 1)
                for t, r in enumerate(TAIL):
                    sp.dma_start(hm_dram[G, 0:r, t * 2 * F:(t + 1) * 2 * F], hm[0:r, G % 2, t, :]).then_inc(stored[G % 2], 16)
                sp.wait_ge(zeroed, 16 * (G + 1))
                sp.wait_ge(stored[G % 2], 16 * ((G + 1) // 2 + len(TAIL)))
                sp.wait_ge(stored[1 - G % 2], 16 * (G // 2))

            @block.gpsimd
            def _(pool):
                pool.memset(idx_raw[:, :, :], 0).then_inc(c_idx, 1)
                pool.memset(ident[:, :], 0.0).then_inc(c_ident, 1)
                pool.wait_ge(c_ident, 1)
                pool.affine_select(out=ident[:, :], in_=ident[:, :], compare_op=ALU.not_equal, fill=1.0, base=0,
                                   pattern=[[-1, P]], channel_multiplier=1).then_inc(c_ident, 1)
                pool.memset(zero[:, :], 0.0).then_inc(c_zero, 1)
                pool.memset(ones[:, :], 1.0).then_inc(c_ones, 1)

                def gather(g, slot):
                    n = len(rows_of(g))
                    pool.tensor_copy(cur[:, slot, :, 0:n], idx[:, :, bass.ds(g * TG, n)]).then_inc(cur_ready, 1)
                    pool.wait_ge(cur_ready, g + 1)
                    pass_waits(pool, "pool")
                    for kind in range(2):
                        for t, r in enumerate(rows_of(g)):
                            pool.indirect_dma_start(
                                out=land[0:r, slot, kind, t, :], out_offset=None, in_=x,
                                in_offset=bass.IndirectOffsetOnAxis(ap=cur[0:r, slot, kind, t:t + 1], axis=0)
                            ).then_inc(land_x[slot], 16)

                pool.wait_ge(idx_ready, 3)
                gather(0, 0)
                gather(1, 1)
                pool.memset(before[:, :], 1.0).then_inc(c_mask, 1)
                pool.wait_ge(c_mask, 1)
                pool.affine_select(out=before[:, GE - P:GE], in_=before[:, GE - P:GE], compare_op=ALU.is_gt, fill=0.0,
                                   base=0, pattern=[[-1, P]], channel_multiplier=1).then_inc(c_mask, 1)
                pool.memset(acc[:, :, :, :], 0.0).then_inc(c_acc, 1)
                pool.iota(lane[:, :, :], pattern=[[0, G + 1], [P, TG]], base=N, channel_multiplier=1).then_inc(lane_made, 1)
                pool.wait_ge(c_acc, 1)

                def body(g, slot, turn):
                    if not (isinstance(g, int) and g + 2 > G):
                        pool.wait_ge(turned, KC * g + KC)
                        gather(g + 2, slot)
                    rows = rows_of(g)
                    pool.wait_ge(taken[H], g * 2 + (2 if len(rows) == TG else 1))
                    if not (isinstance(g, int) and g == 0):
                        pool.wait_ge(summed, g * 2)
                    if len(rows) == TG:
                        parts = [(P, slice(0, TG))]
                    else:
                        parts = [(r, slice(t, t + 1)) for t, r in enumerate(rows)]
                    for r, ts in parts:
                        last = pool.tensor_tensor(acc[0:r, 0, ts, :], acc[0:r, 0, ts, :], hm[0:r, slot, ts, 0:F], ALU.add)
                    last.then_inc(summed, 1)
                    pool.wait_ge(squared, g + 1)
                    for r, ts in parts:
                        last = pool.tensor_tensor(acc[0:r, 1, ts, :], acc[0:r, 1, ts, :], hsq[0:r, ts, :], ALU.add)
                    last.then_inc(summed, 1)

                in_order(pool, body, [(0, 1), (1, G - 4), (G - 3, 1), (G - 2, 3)], 2)

            @block.scalar
            def _(act):
                for u, (layer, b, k) in enumerate(units):
                    act.wait_ge(w_turned, u + 1)
                    to = (w1hl if layer == 1 else w2hl)[0][:, b, k, :]
                    act.activation(to, bank[:, TURN + u % 2, 0:F], ACT.Copy).then_inc(w_hi, 1)
                act.wait_ge(vec_in, 16 * 8)

                def round_chunk(g, k):
                    n = GE if len(rows_of(g)) == TG else REST
                    act.wait_ge(turned, KC * g + k + 1)
                    if not (isinstance(g, int) and g == 0):
                        act.wait_ge(l1n_step, KC * g + (k + 1 - KC))
                    act.activation(xT[0][:, k, 0:n], bank[:, TURN + k % 2, 0:n], ACT.Copy).then_inc(hi_ready, 1)

                def silu(g, b):
                    n = GE if len(rows_of(g)) == TG else REST
                    if b == H:
                        act.wait_ge(l1h_done, g + 1)
                    else:
                        act.wait_ge(l1n_step, KC * g + KC)
                    for c in range(MC):
                        if not (isinstance(g, int) and g == 0 and b == H):
                            act.wait_ge(glo_ready, 4 * g + 2 * b + c - 1)
                        act.activation(g32[:, c, 0:n], bank[:, bank_of[b][c], 0:n], ACT.Silu,
                                       bias=b1c[:, b, c:c + 1]).then_inc(silu_done, 1)

                def square(g, slot):
                    rows = rows_of(g)
                    act.wait_ge(taken[H], g * 2 + (2 if len(rows) == TG else 1))
                    if not (isinstance(g, int) and g == 0):
                        act.wait_ge(summed, g * 2)
                    if len(rows) == TG:
                        last = act.activation(hsq[:, :, :], hm[:, slot, :, 0:F], ACT.Square)
                    else:
                        for t, r in enumerate(rows):
                            last = act.activation(hsq[0:r, t, :], hm[0:r, slot, t, 0:F], ACT.Square)
                    last.then_inc(squared, 1)

                def body(g, slot, turn):
                    silu(g, H)
                    if not (isinstance(g, int) and g == G):
                        for k in range(KC):
                            round_chunk(g + 1, k)
                    silu(g, M)
                    square(g, slot)

                for k in range(KC):
                    round_chunk(0, k)
                in_order(act, body, [(0, 1), (1, G - 2), (G - 1, 2)], 2)
                bn_std(act, bn1_var, bn1_std)

            @block.vector
            def _(dve):
                dve.wait_ge(idx_in, 64)
                dve.tensor_copy(idx_f[:, :, :], idx_raw[:, :, :]).then_inc(idx_float, 1)
                dve.wait_ge(idx_turned, 1)
                for i in range(2):
                    dve.tensor_copy(idx[:, i, 0:NT], bank[:, 0, i * P:i * P + NT]).then_inc(idx_ready, 1)
                dve.tensor_copy(dst_col[:, 0:NT], bank[:, 0, 0:NT]).then_inc(idx_ready, 1)
                dve.memset(earlier[:, :], 0.0).then_inc(idx_ready, 1)
                for u, (layer, b, k) in enumerate(units):
                    dve.wait_ge(w_hi, u + 1)
                    hl = w1hl if layer == 1 else w2hl
                    dve.tensor_tensor(hl[1][:, b, k, :], bank[:, TURN + u % 2, 0:F],
                                      hl[0][:, b, k, :].bitcast(F32), ALU.subtract).then_inc(w_lo, 1)
                dve.wait_ge(vec_in, 16 * 8)

                def rest_chunk(g, k):
                    n = GE if len(rows_of(g)) == TG else REST
                    dve.wait_ge(hi_ready, KC * g + k + 1)
                    dve.tensor_tensor(xT[1][:, k, 0:n], bank[:, TURN + k % 2, 0:n],
                                      xT[0][:, k, 0:n].bitcast(F32), ALU.subtract).then_inc(lo_ready, 1)

                def split(g, b):
                    n = GE if len(rows_of(g)) == TG else REST
                    if not (isinstance(g, int) and g == 0):
                        dve.wait_ge(l2_done[b], g * 2)
                    for c in range(MC):
                        dve.wait_ge(silu_done, 4 * g + 2 * b + c + 1)
                        dve.tensor_copy(g_hl[0][:, b, c, 0:n], g32[:, c, 0:n]).then_inc(ghi_ready, 1)
                    for c in range(MC):
                        dve.wait_ge(ghi_ready, 4 * g + 2 * b + c + 1)
                        dve.tensor_tensor(g_hl[1][:, b, c, 0:n], g32[:, c, 0:n],
                                          g_hl[0][:, b, c, 0:n].bitcast(F32), ALU.subtract).then_inc(glo_ready, 1)

                def take(g, b, slot):
                    rows = rows_of(g)
                    if b == H and not (isinstance(g, int) and g < 2):
                        dve.wait_ge(summed, g * 2 - 2)
                        dve.wait_ge(stored[slot], stored_before(g))
                    if len(rows) == TG:
                        for q in range(2):
                            dve.wait_ge(l2_done[b], g * 2 + q + 1)
                            dve.tensor_tensor(hm[:, slot, 2 * q:2 * q + 2, b * F:(b + 1) * F],
                                              bank[:, L2 + q, :].rearrange("p (t f) -> p t f", t=2),
                                              b2b[:, b, :].unsqueeze(1).to_broadcast([P, 2, F]), ALU.add).then_inc(taken[b], 1)
                    else:
                        dve.wait_ge(l2_done[b], g * 2 + 1)
                        for t, r in enumerate(rows):
                            last = dve.tensor_tensor(hm[0:r, slot, t, b * F:(b + 1) * F], bank[0:r, L2, t * F:(t + 1) * F],
                                                     b2b[0:r, b, :], ALU.add)
                        last.then_inc(taken[b], 1)

                turn_of = {}

                def stored_before(g):
                    return 16 * g // 2 if isinstance(g, int) and g % 2 == 0 else \
                        16 * ((g - 1) // 2) if isinstance(g, int) else turn_of["turn"] * 16

                def count_earlier(g, slot, turn):
                    rows = rows_of(g)
                    dve.wait_ge(drow_in[slot], turn * 16 + 16)
                    if not (isinstance(g, int) and g == 0):
                        dve.wait_ge(counted, g)
                    at = 0
                    for a, r in enumerate(rows):
                        n = min((a + 1) * P, GE if len(rows) == TG else REST)
                        last = dve.scalar_tensor_tensor(
                            out=scratch[0:r, at:at + n], in0=drow[0:r, slot, 0:n],
                            scalar=dst_col[0:r, bass.ds(g * TG + a, 1)], in1=before[0:r, GE - P - a * P:GE - P - a * P + n],
                            op0=ALU.is_equal, op1=ALU.mult, accum_out=earlier[0:r, bass.ds(g * TG + a, 1)])
                        at += n
                    last.then_inc(counted, 1)

                def body(g, slot, turn):
                    turn_of["turn"] = turn
                    split(g, H)
                    if not (isinstance(g, int) and g == 0):
                        take(g - 1, M, 1 - slot)
                    if not (isinstance(g, int) and g == G):
                        for k in range(KC):
                            rest_chunk(g + 1, k)
                    split(g, M)
                    take(g, H, slot)
                    count_earlier(g, slot, turn)

                for k in range(KC):
                    rest_chunk(0, k)
                dve.wait_ge(c_mask, 2)
                dve.wait_ge(idx_ready, 4)
                in_order(dve, body, [(0, 1), (1, G - 2), (G - 1, 2)], 2)
                take(G, M, G % 2)
                dve.wait_ge(lane_made, 1)
                dve.wait_ge(counted, G + 1)
                steps = [
                    lambda: dve.tensor_copy(lane_f[:, :], lane[:, :, :].rearrange("p g t -> p (g t)")),
                    lambda: dve.tensor_scalar(dup[:, :], earlier[:, :], 0.0, None, ALU.is_gt),
                    lambda: dve.tensor_tensor(lane_f[:, 0:NT], lane_f[:, 0:NT], dst_col[:, 0:NT], ALU.subtract),
                    lambda: dve.tensor_tensor(lane_f[:, 0:NT], lane_f[:, 0:NT], dup[:, 0:NT], ALU.mult),
                    lambda: dve.tensor_tensor(scatter_idx[:, 0:NT], lane_f[:, 0:NT], dst_col[:, 0:NT], ALU.add),
                ]
                for i, s in enumerate(steps):
                    s().then_inc(idx_step, 1)
                    dve.wait_ge(idx_step, i + 1)
                dve.wait_ge(stats_done, 1)
                bn_coefficients(dve, 0, bank[:, 0, 0:F], bank[:, 1, 0:F], E, bn1, bn1_var, bn1_std)

            @block.tensor
            def _(pe):
                pe.wait_ge(idx_float, 1)
                pe.wait_ge(c_ident, 2)
                for i in range(2):
                    last = pe.transpose(bank[:, 0, i * P:i * P + NT], idx_f[0:NT, i, :], ident[0:NT, 0:NT])
                last.then_inc(idx_turned, 1)
                pe.wait_ge(w_in, 64)
                for u, (layer, b, k) in enumerate(units):
                    if u >= 2:
                        pe.wait_ge(w_lo, u - 1)
                    for c in range(MC):
                        raw = (w1_raw if layer == 1 else w2_raw)[:, b, c, k * P:(k + 1) * P]
                        last = pe.transpose(bank[:, TURN + u % 2, c * P:(c + 1) * P], raw, ident[:, :])
                    last.then_inc(w_turned, 1)

                def turn_chunk(g, k, slot, turn):
                    rows = rows_of(g)
                    n_in = 8 if len(rows) == TG else 2 * len(rows)
                    if k == 0:
                        pe.wait_ge(land_x[slot], turn * 128 + 16 * n_in)
                    if k == 2 * F // P:
                        pe.wait_ge(land_e[slot], turn * 16 + (16 if len(rows) == TG else 32))
                    if not (isinstance(g, int) and g == 0 and k < 2):
                        pe.wait_ge(lo_ready, KC * g + k - 1)
                    kind, half = divmod(k, F // P)
                    for t, r in enumerate(rows):
                        last = pe.transpose(bank[:, TURN + k % 2, t * P:t * P + r],
                                            land[0:r, slot, kind, t, half * P:(half + 1) * P], ident[0:r, 0:r])
                    last.then_inc(turned, 1)

                def layer1(g, b, k):
                    n = GE if len(rows_of(g)) == TG else REST
                    if k == 0 and not (isinstance(g, int) and g == 0):
                        pe.wait_ge(silu_done, 4 * g + (2 * b - 2))
                    if b == H:
                        pe.wait_ge(lo_ready, KC * g + k + 1)
                    for c in range(MC):
                        for j, (w, v) in enumerate(((0, 0), (0, 1), (1, 0))):
                            last = pe.matmul(bank[:, bank_of[b][c], 0:n], w1hl[w][:, b, k, c * P:(c + 1) * P],
                                             xT[v][:, k, 0:n], start=(k == 0 and j == 0), stop=(k == KC - 1 and j == 2))
                    if b == M:
                        last.then_inc(l1n_step, 1)
                    elif k == KC - 1:
                        last.then_inc(l1h_done, 1)

                def layer2(g, b):
                    rows = rows_of(g)
                    pe.wait_ge(glo_ready, 4 * g + 2 * b + 2)
                    for t, r in enumerate(rows):
                        if t % 2 == 0:
                            if b == M:
                                pe.wait_ge(taken[H], g * 2 + 1 + t // 2)
                            elif not (isinstance(g, int) and g == 0):
                                pe.wait_ge(taken[M], g * 2 - 1 + t // 2)
                        n = 0
                        for k in range(MC):
                            for v, w in ((0, 0), (0, 1), (1, 0)):
                                last = pe.matmul(bank[0:r, L2 + t // 2, (t % 2) * F:(t % 2 + 1) * F],
                                                 g_hl[v][:, b, k, t * P:t * P + r], w2hl[w][:, b, k, :],
                                                 start=(n == 0), stop=(n == 3 * MC - 1))
                                n += 1
                        if t % 2 == 1:
                            last.then_inc(l2_done[b], 1)

                def body(g, slot, turn):
                    for k in range(KC):
                        layer1(g, H, k)
                    if not (isinstance(g, int) and g == 0):
                        layer2(g - 1, M)
                    for k in range(KC):
                        layer1(g, M, k)
                        if not (isinstance(g, int) and g == G):
                            turn_chunk(g + 1, k, 1 - slot, turn + slot)
                    layer2(g, H)

                pe.wait_ge(w_lo, len(units))
                for k in range(KC):
                    turn_chunk(0, k, 0, 0)
                in_order(pe, body, [(0, 1), (1, G - 2), (G - 1, 2)], 2)
                layer2(G, M)
                pe.wait_ge(c_ones, 1)
                pe.wait_ge(summed, 2 * G + 2)
                for i in range(2):
                    for t in range(TG):
                        last = pe.matmul(bank[:, i, 0:F], ones[:, :], acc[:, i, t, :], start=(t == 0), stop=(t == TG - 1))
                last.then_inc(stats_done, 1)

        with ExitStack() as s2:
            def sb(name, shape, dt=F32):
                return s2.enter_context(nc.sbuf_tensor(name, shape, dt))
            R2 = 4
            hm2 = sb("hm2", [P, R2, TG, 2 * F])
            drow2 = sb("drow2", [P, R2, GE], I32)
            score = sb("score", [P, 2, TG, F])
            msg = sb("msg", [P, 2, TG, F])
            same = sb("same", [P, 2, 10 * P])
            sums = sb("sums", [P, 2, TG, F])
            cur2 = sb("cur2", [P, 2, TG], I32)
            group_in = [sem(f"group_in{i}") for i in range(R2)]
            scaled, shifted, scored, msg_ready = sem("scaled"), sem("shifted"), sem("scored"), sem("msg_ready")
            combined, sums_ready, added = sem("combined"), sem("sums_ready"), sem("added")
            cur2_ready = sem("cur2_ready")
            same_at = [sum(range(b + 1)) * P for b in range(TG)]
            block = s2.enter_context(nc.Block())

            def is_first(g, n=1):
                return isinstance(g, int) and g < n

            def parts_of(g):
                rows = rows_of(g)
                return [(P, slice(0, TG))] if len(rows) == TG else [(r, slice(t, t + 1)) for t, r in enumerate(rows)]

            def wide(v, r, n):
                return v.unsqueeze(1).to_broadcast([r, n, F])

            @block.sync
            def _(sp):
                def load(g, slot):
                    rows = rows_of(g)
                    if len(rows) == TG:
                        sp.dma_start(hm2[:, slot, :, :].rearrange("p t n -> p (t n)"),
                                     hm_dram[bass.ds(g, 1), :, :].rearrange("o p n -> (o p) n")).then_inc(group_in[slot], 16)
                        sp.dma_start(drow2[:, slot, :], dst[bass.ds(g * GE, GE)].rearrange("(o n) -> o n", o=1)
                                     .to_broadcast([P, GE])).then_inc(group_in[slot], 16)
                    else:
                        for t, r in enumerate(rows):
                            sp.dma_start(hm2[0:r, slot, t, :], hm_dram[G, 0:r, t * 2 * F:(t + 1) * 2 * F]).then_inc(group_in[slot], 16)
                        sp.dma_start(drow2[:, slot, 0:REST], dst[G * GE:E].rearrange("(o n) -> o n", o=1)
                                     .to_broadcast([P, REST])).then_inc(group_in[slot], 16)

                for g in range(R2):
                    load(g, g)

                def body(g, slot, turn):
                    sp.wait_ge(msg_ready, g + 1)
                    pass_waits(sp, "sp")
                    load(g + R2, slot)
                in_order(sp, body, [(0, G - R2), (G - R2, 1)], R2)

            @block.vector
            def _(dve):
                def front(g, slot, turn):
                    par = slot % 2
                    rows = rows_of(g)
                    n_in = 2 if len(rows) == TG else 1 + len(rows)
                    dve.wait_ge(group_in[slot], turn * 32 + 16 * n_in)
                    if not is_first(g, 2):
                        dve.wait_ge(msg_ready, g - 1)
                        dve.wait_ge(combined, g - 1)
                    for r, ts in parts_of(g):
                        k = TG if len(rows) == TG else 1
                        last = dve.tensor_tensor(score[0:r, par, ts, :], hm2[0:r, slot, ts, 0:F], wide(A[0:r, 0, :], r, k), ALU.mult)
                    last.then_inc(scaled, 1)
                    for b, r in enumerate(rows):
                        n = min((b + 1) * P, GE if len(rows) == TG else REST)
                        dve.tensor_scalar(same[0:r, par, same_at[b]:same_at[b] + n], drow2[0:r, slot, 0:n],
                                          dst_col[0:r, bass.ds(g * TG + b, 1)], None, ALU.is_equal)
                    dve.wait_ge(scaled, g + 1)
                    for r, ts in parts_of(g):
                        k = TG if len(rows) == TG else 1
                        last = dve.tensor_tensor(score[0:r, par, ts, :], score[0:r, par, ts, :], wide(Bc[0:r, 0, :], r, k), ALU.add)
                    last.then_inc(shifted, 1)

                def back(g, slot):
                    dve.wait_ge(scored, g + 1)
                    for r, ts in parts_of(g):
                        last = dve.tensor_tensor(msg[0:r, slot % 2, ts, :], score[0:r, slot % 2, ts, :],
                                                 hm2[0:r, slot, ts, F:2 * F], ALU.mult)
                    last.then_inc(msg_ready, 1)

                def body(g, slot, turn):
                    if not (isinstance(g, int) and g == G):
                        front(g + 1, (slot + 1) % R2, turn + (slot + 1) // R2)
                    back(g, slot)
                front(0, 0, 0)
                in_order(dve, body, [(0, 1), (1, G - 4), (G - 3, 4)], R2)

            @block.scalar
            def _(act):
                def score_of(g, slot):
                    act.wait_ge(shifted, g + 1)
                    for r, ts in parts_of(g):
                        last = act.activation(score[0:r, slot % 2, ts, :], score[0:r, slot % 2, ts, :], ACT.Sigmoid)
                    last.then_inc(scored, 1)

                def body(g, slot, turn):
                    if not (isinstance(g, int) and g == G):
                        score_of(g + 1, (slot + 1) % 2)
                    par = slot % 2
                    act.wait_ge(combined, g + 1)
                    if not is_first(g, 2):
                        act.wait_ge(added, 64 * g - 64)
                    for r, ts in parts_of(g):
                        k = TG if len(rows_of(g)) == TG else 1
                        last = act.activation(sums[0:r, par, ts, :],
                                              bank[0:r, 2 * par:2 * par + 2, :].rearrange("p b (t f) -> p (b t) f", t=2)[:, ts, :],
                                              ACT.Copy)
                    last.then_inc(sums_ready, 1)
                score_of(0, 0)
                in_order(act, body, [(0, 2), (2, G - 4), (G - 2, 3)], 2)

            @block.tensor
            def _(pe):
                def body(g, slot, turn):
                    rows = rows_of(g)
                    pe.wait_ge(msg_ready, g + 1)
                    if not is_first(g, 2):
                        pe.wait_ge(sums_ready, g - 1)
                    for a, ra in enumerate(rows):
                        for b in range(a, len(rows)):
                            last = pe.matmul(bank[0:ra, 2 * slot + a // 2, (a % 2) * F:(a % 2 + 1) * F],
                                             same[0:rows[b], slot, same_at[b] + a * P:same_at[b] + a * P + ra],
                                             msg[0:rows[b], slot, b, :], start=(b == a), stop=(b == len(rows) - 1))
                    last.then_inc(combined, 1)
                in_order(pe, body, [(0, 2), (2, G - 2), (G, 1)], 2)

            @block.gpsimd
            def _(pool):
                def body(g, slot, turn):
                    rows = rows_of(g)
                    if not is_first(g, 1):
                        pool.wait_ge(added, 64 * g)
                    pool.tensor_copy(cur2[:, slot, 0:len(rows)], scatter_idx[:, bass.ds(g * TG, len(rows))]).then_inc(cur2_ready, 1)
                    pool.wait_ge(cur2_ready, g + 1)
                    pass_waits(pool, "pool")
                    pool.wait_ge(sums_ready, g + 1)
                    pass_waits(pool, "pool")
                    for t, r in enumerate(rows):
                        pool.indirect_dma_start(
                            out=table, out_offset=bass.IndirectOffsetOnAxis(ap=cur2[0:r, slot, t:t + 1], axis=0),
                            in_=sums[0:r, slot, t, :], in_offset=None, compute_op=ALU.add).then_inc(added, 16)
                in_order(pool, body, [(0, 1), (1, G - 2), (G - 1, 2)], 2)
                pool.wait_ge(added, 64 * G + 16 * len(TAIL))

        with ExitStack() as s3:
            def sb(name, shape, dt=F32):
                return s3.enter_context(nc.sbuf_tensor(name, shape, dt))
            R = 3
            RT = 2 * R
            W = RJ * F
            assert RES % RT == 0
            res = sb("res", [P, RES, W])
            tr = sb("tr", [P, RT, W])
            xr = sb("xr", [P, R, W])
            ob = sb("ob", [P, R, W])
            unread = sb("unread", [P, W], mybir.dt.bfloat16)
            tail_t = sb("tail_t", [P, F])
            tail_x = sb("tail_x", [P, F])
            tail_o = sb("tail_o", [P, F])
            row_sum = sb("row_sum", [P, RT, RJ])
            row_sq = sb("row_sq", [P, RT, RJ])
            row_mean = sb("row_mean", [P, RT, RJ])
            row_var = sb("row_var", [P, RT, RJ])
            row_rstd = sb("row_rstd", [P, RT, RJ])
            row_shift = sb("row_shift", [P, RT, RJ])

            table_v = table[0:NMAIN, :].rearrange("(p c j) f -> p c (j f)", p=P, c=C)
            x_v = x[0:NMAIN, :].rearrange("(p c j) f -> p c (j f)", p=P, c=C)
            out_v = out[0:NMAIN, :].rearrange("(p c j) f -> p c (j f)", p=P, c=C)
            acc2 = xr[:, 0, :]

            def chunk(v, c):
                return v[:, bass.ds(c, 1), :].rearrange("p o n -> p (o n)")

            ahead = (RES - 1 - 3) // RT * RT
            PIECES = [(0, 3), (3, ahead), (3 + ahead, RES - 1 - ahead),
                      (RES + 2, (C - 1 - RES - 2) // RT * RT)]
            PIECES.append((sum(PIECES[-1]), C - sum(PIECES[-1])))
            stays = {}

            def chunks_in_order(eng, body):
                for first, count in PIECES:
                    stays["now"] = first < RES
                    in_order(eng, body, [(first, count)], RT)

            def in_res(c):
                return c < RES if isinstance(c, int) else stays["now"]

            def kept(c, slot, part=slice(0, W)):
                if in_res(c):
                    return res[:, bass.ds(c, 1), part].rearrange("p o n -> p (o n)")
                return tr[:, slot % RT, part]

            def row(j):
                return slice(j * F, (j + 1) * F)

            with ExitStack() as sums_block:
                t_in = [sem(f"t_in{i}") for i in range(RT)]
                tail_in, sq_ready, sq_summed = sem("tail_in"), sem("sq_ready"), sem("sq_summed")
                col_summed, tail_sq, sq_zero = sem("col_summed"), sem("tail_sq"), sem("sq_zero")
                cols_ready, bn2, bn2_var, bn2_std = sem("cols_ready"), sem("bn2"), sem("bn2_var"), sem("bn2_std")
                block = sums_block.enter_context(nc.Block())

                @block.sync
                def _(sp):
                    sp.dma_start(tail_t[0:NTAIL, :], table[NMAIN:N, :]).then_inc(tail_in, 16)
                    sp.dma_start(tail_x[0:NTAIL, :], x[NMAIN:N, :]).then_inc(tail_in, 16)

                    def body(c, slot, turn):
                        if not is_first(c, RT):
                            sp.wait_ge(sq_ready, c - RT + 1)
                            sp.wait_ge(col_summed, c - RT + 1)
                            pass_waits(sp, "sp")
                        sp.dma_start(kept(c, slot), chunk(table_v, c)).then_inc(t_in[slot], 16)
                    stays["now"] = True
                    in_order(sp, body, [(0, RT), (RT, RES - RT)], RT)
                    stays["now"] = False
                    in_order(sp, body, [(RES, C - RES)], RT)

                @block.scalar
                def _(act):
                    def body(c, slot, turn):
                        act.wait_ge(t_in[slot], turn * 16 + 16)
                        if not is_first(c, R):
                            act.wait_ge(sq_summed, c - R + 1)
                        pass_waits(act, "act")
                        act.activation(ob[:, slot % R, :], kept(c, slot), ACT.Square).then_inc(sq_ready, 1)
                    chunks_in_order(act, body)
                    act.wait_ge(tail_in, 32)
                    act.activation(tail_o[0:NTAIL, :], tail_t[0:NTAIL, :], ACT.Square).then_inc(tail_sq, 1)
                    bn_std(act, bn2_var, bn2_std)

                @block.vector
                def _(dve):
                    dve.memset(acc2, 0.0).then_inc(sq_zero, 1)
                    dve.wait_ge(sq_zero, 1)

                    def body(c, slot, turn):
                        dve.wait_ge(sq_ready, c + 1)
                        if not is_first(c, 1):
                            dve.wait_ge(sq_summed, c)
                        dve.tensor_tensor(acc2, acc2, ob[:, slot % R, :], ALU.add).then_inc(sq_summed, 1)
                    chunks_in_order(dve, body)
                    dve.wait_ge(cols_ready, 1)
                    bn_coefficients(dve, 1, bank[:, 0, 0:F], bank[:, 1, 0:F], N, bn2, bn2_var, bn2_std)

                @block.tensor
                def _(pe):
                    def body(c, slot, turn):
                        pe.wait_ge(t_in[slot], turn * 16 + 16)
                        for j in range(RJ):
                            last = pe.matmul(bank[:, 0, 0:F], ones[:, :], kept(c, slot, row(j)),
                                             start=(is_first(c, 1) and j == 0), stop=False)
                        last.then_inc(col_summed, 1)
                    chunks_in_order(pe, body)
                    pe.wait_ge(tail_in, 32)
                    pe.matmul(bank[:, 0, 0:F], ones[0:NTAIL, :], tail_t[0:NTAIL, :], start=False, stop=True)
                    pe.wait_ge(tail_sq, 1)
                    pe.matmul(bank[:, 1, 0:F], ones[0:NTAIL, :], tail_o[0:NTAIL, :], start=True, stop=False)
                    pe.wait_ge(sq_summed, C)
                    for j in range(RJ):
                        last = pe.matmul(bank[:, 1, 0:F], ones[:, :], acc2[:, row(j)], start=False, stop=(j == RJ - 1))
                    last.then_inc(cols_ready, 1)

            x_in = [sem(f"x_in{i}") for i in range(R)]
            t_again = [sem(f"t_again{i}") for i in range(RT)]
            xb_ready, t_scaled, z_ready = sem("xb_ready"), sem("t_scaled"), sem("z_ready")
            y_ready, y_squared, small = sem("y_ready"), sem("y_squared"), sem("small")
            var_ready, std_ready, inverse, coef, normed = sem("var_ready"), sem("std_ready"), sem("inverse"), sem("coef"), sem("normed")
            out_done = [sem(f"out_done{i}") for i in range(R)]
            tail_ready, tail_stored, tail_step, tail_std = sem("tail_ready"), sem("tail_stored"), sem("tail_step"), sem("tail_std")
            tail_var = sem("tail_var")
            block = s3.enter_context(nc.Block())
            XB = [0, 3]

            @block.sync
            def _(sp):
                def put(c, slot):
                    sp.wait_ge(normed, c + 1)
                    pass_waits(sp, "sp")
                    sp.dma_start(chunk(out_v, c), ob[:, slot % R, :]).then_inc(out_done[slot % R], 16)

                def body(c, slot, turn):
                    if not is_first(c, R):
                        sp.wait_ge(y_ready, c - R + 1)
                        pass_waits(sp, "sp")
                    sp.dma_start(xr[:, slot % R, :], chunk(x_v, c)).then_inc(x_in[slot % R], 16)
                    if not in_res(c):
                        sp.wait_ge(normed, c - RT + 1)
                        pass_waits(sp, "sp")
                        sp.dma_start(tr[:, slot, :], chunk(table_v, c)).then_inc(t_again[slot], 16)
                    if not is_first(c, 3):
                        put(c - 3, (slot + RT - 3) % RT)
                chunks_in_order(sp, body)
                for c in range(C - 3, C):
                    put(c, c % RT)
                sp.wait_ge(tail_ready, 1)
                sp.dma_start(out[NMAIN:N, :], tail_o[0:NTAIL, :]).then_inc(tail_stored, 16)
                sp.wait_ge(tail_stored, 16)
                for i in range(R):
                    sp.wait_ge(out_done[i], 16 * ((C - i + R - 1) // R))

            @block.tensor
            def _(pe):
                def body(c, slot, turn):
                    pe.wait_ge(x_in[slot % R], turn * 32 + 16 * (slot // R) + 16)
                    if not is_first(c, 2):
                        pe.wait_ge(z_ready, c - 1)
                    for j in range(RJ):
                        o = bank[:, XB[slot % 2] + j // 2, (j % 2) * F:(j % 2 + 1) * F]
                        pe.matmul(o, ident[:, :], xr[:, slot % R, row(j)], start=True, stop=False)
                        last = pe.matmul(o, ones[0:1, :], Bc[0:1, 1, :], start=False, stop=True)
                    last.then_inc(xb_ready, 1)
                in_order(pe, body, [(0, 2), (2, C - 2)], RT)

            @block.vector
            def _(dve):
                def scale(c, slot, turn):
                    if not in_res(c):
                        dve.wait_ge(t_again[slot], (turn - RES // RT) * 16 + 16)
                    t = kept(c, slot).rearrange("p (j f) -> p j f", f=F)
                    dve.tensor_tensor(t, t, A[:, 1, :].unsqueeze(1).to_broadcast([P, RJ, F]), ALU.mult).then_inc(t_scaled, 1)

                def add(c, slot):
                    dve.wait_ge(t_scaled, c + 1)
                    dve.wait_ge(xb_ready, c + 1)
                    b0 = XB[slot % 2]
                    dve.tensor_tensor(kept(c, slot), kept(c, slot),
                                      bank[:, b0:b0 + 3, :].rearrange("p b n -> p (b n)")[:, 0:W], ALU.add).then_inc(z_ready, 1)

                def relu_add(c, slot):
                    dve.wait_ge(z_ready, c + 1)
                    for j in range(RJ):
                        y = kept(c, slot, row(j))
                        last = dve.scalar_tensor_tensor(out=y, in0=y, scalar=0.0, in1=xr[:, slot % R, row(j)],
                                                        op0=ALU.max, op1=ALU.add, accum_out=row_sum[:, slot, j:j + 1])
                    last.then_inc(y_ready, 1)

                def variance(c, slot):
                    dve.wait_ge(y_squared, c + 1)
                    mean, var = row_mean[:, slot, :], row_var[:, slot, :]
                    dve.tensor_scalar(mean, row_sum[:, slot, :], 1.0 / F, None, ALU.mult).then_inc(small, 1)
                    dve.wait_ge(small, 3 * c + 1)
                    dve.tensor_tensor(var, mean, mean, ALU.mult).then_inc(small, 1)
                    dve.wait_ge(small, 3 * c + 2)
                    dve.scalar_tensor_tensor(out=var, in0=row_sq[:, slot, :], scalar=1.0 / F, in1=var,
                                             op0=ALU.mult, op1=ALU.subtract).then_inc(small, 1)
                    dve.wait_ge(small, 3 * c + 3)
                    dve.tensor_scalar(var, var, 0.0, EPS, ALU.max, ALU.add).then_inc(var_ready, 1)

                def invert(c, slot):
                    dve.wait_ge(std_ready, c + 1)
                    dve.reciprocal(row_rstd[:, slot, :], row_var[:, slot, :]).then_inc(inverse, 1)
                    dve.wait_ge(inverse, c + 1)
                    dve.scalar_tensor_tensor(out=row_shift[:, slot, :], in0=row_mean[:, slot, :], scalar=-1.0,
                                             in1=row_rstd[:, slot, :], op0=ALU.mult, op1=ALU.mult).then_inc(coef, 1)

                def body(c, slot, turn):
                    if not (isinstance(c, int) and c == C - 1):
                        scale(c + 1, (slot + 1) % RT, turn + (slot + 1) // RT)
                    if not is_first(c, 2):
                        invert(c - 2, (slot + RT - 2) % RT)
                    add(c, slot)
                    relu_add(c, slot)
                    if not is_first(c, 1):
                        variance(c - 1, (slot + RT - 1) % RT)
                scale(0, 0, 0)
                chunks_in_order(dve, body)
                invert(C - 2, (C - 2) % RT)
                variance(C - 1, (C - 1) % RT)
                invert(C - 1, (C - 1) % RT)
                n = NTAIL
                s = [0]

                def link(ins):
                    s[0] += 1
                    ins.then_inc(tail_step, 1)
                    dve.wait_ge(tail_step, s[0])
                dve.wait_ge(normed, C)
                total, squares, mean, var, rstd = (v[0:n, 0, 0:1] for v in (row_sum, row_sq, row_mean, row_var, row_rstd))
                tt = tail_t[0:n, :]
                link(dve.tensor_tensor(tt, tt, A[0:n, 1, :], ALU.mult))
                link(dve.tensor_tensor(tt, tt, Bc[0:n, 1, :], ALU.add))
                link(dve.tensor_tensor(tt, tt, tail_x[0:n, :], ALU.add))
                link(dve.scalar_tensor_tensor(out=tt, in0=tt, scalar=0.0, in1=tail_x[0:n, :],
                                              op0=ALU.max, op1=ALU.add, accum_out=total))
                link(dve.scalar_tensor_tensor(out=tail_o[0:n, :], in0=tt, scalar=1.0, in1=tt,
                                              op0=ALU.mult, op1=ALU.mult, accum_out=squares))
                link(dve.tensor_scalar(mean, total, 1.0 / F, None, ALU.mult))
                link(dve.tensor_tensor(var, mean, mean, ALU.mult))
                link(dve.scalar_tensor_tensor(out=var, in0=squares, scalar=1.0 / F, in1=var, op0=ALU.mult, op1=ALU.subtract))
                dve.tensor_scalar(var, var, 0.0, EPS, ALU.max, ALU.add).then_inc(tail_var, 1)
                dve.wait_ge(tail_std, 1)
                link(dve.reciprocal(rstd, var))
                link(dve.tensor_scalar(tt, tt, mean, None, ALU.subtract))
                dve.tensor_scalar(tail_o[0:n, :], tt, rstd, None, ALU.mult).then_inc(tail_ready, 1)

            @block.scalar
            def _(act):
                def squares(c, slot):
                    act.wait_ge(y_ready, c + 1)
                    if not is_first(c, 1):
                        act.wait_ge(y_squared, c)
                    pass_waits(act, "act")
                    for j in range(RJ):
                        last = act.activation(unread[:, row(j)], kept(c, slot, row(j)), ACT.Square,
                                              accum_out=row_sq[:, slot, j:j + 1])
                    last.then_inc(y_squared, 1)

                def root(c, slot):
                    act.wait_ge(var_ready, c + 1)
                    act.activation(row_var[:, slot, :], row_var[:, slot, :], ACT.Sqrt).then_inc(std_ready, 1)

                def norm(c, slot, turn):
                    act.wait_ge(coef, c + 1)
                    if not is_first(c, R):
                        act.wait_ge(out_done[slot % R], turn * 32 + 16 * (slot // R))
                    pass_waits(act, "act")
                    for j in range(RJ):
                        last = act.activation(ob[:, slot % R, row(j)], kept(c, slot, row(j)), ACT.Identity,
                                              bias=row_shift[:, slot, j:j + 1], scale=row_rstd[:, slot, j:j + 1])
                    last.then_inc(normed, 1)

                def body(c, slot, turn):
                    squares(c, slot)
                    if not is_first(c, 1):
                        root(c - 1, (slot + RT - 1) % RT)
                    if not is_first(c, 2):
                        norm(c - 2, (slot + RT - 2) % RT, turn - (1 if slot < 2 else 0))
                chunks_in_order(act, body)
                norm(C - 2, (C - 2) % RT, (C - 2) // RT)
                root(C - 1, (C - 1) % RT)
                norm(C - 1, (C - 1) % RT, (C - 1) // RT)
                act.wait_ge(tail_var, 1)
                v = row_var[0:NTAIL, 0, 0:1]
                act.activation(v, v, ACT.Sqrt).then_inc(tail_std, 1)


_INS = ['x', 'src', 'dst', 'edge_attr_256', 'L0_gnn_w_full1', 'L0_gnn_b_full1', 'L0_gnn_w_full2', 'L0_gnn_b_full2',
        'L0_gnn_w_n1', 'L0_gnn_b_n1', 'L0_gnn_w_n2', 'L0_gnn_b_n2', 'L0_gnn_gamma_int', 'L0_gnn_beta_int',
        'L0_gnn_gamma_bn', 'L0_gnn_beta_bn']


def kernel(**inputs):
    import numpy as np
    import concourse.bacc as bacc
    from concourse.bass_utils import run_bass_kernel_spmd

    nc = bacc.Bacc("TRN2", target_bir_lowering=False, num_devices=1)
    arrays, args = {}, []
    for name in _INS:
        a = np.ascontiguousarray(inputs[name])
        arrays[f"in_{name}"] = a
        args.append(nc.dram_tensor(f"in_{name}", a.shape, mybir.dt.from_np(a.dtype), kind="ExternalInput").ap())
    shape = inputs['x'].shape
    args.append(nc.dram_tensor("out_rows", shape, F32, kind="ExternalOutput").ap())
    gnn_program(nc, *args)
    r = run_bass_kernel_spmd(nc, [arrays], core_ids=[0])
    return r.results[0]["out_rows"]
```

```python
from contextlib import ExitStack

import concourse.bass as bass
from concourse import mybir

F32 = mybir.dt.float32
F32R = mybir.dt.float32r
I32 = mybir.dt.int32
ALU = mybir.AluOpType
ACT = mybir.ActivationFunctionType

P = 128
EPS = 1e-5


def in_order(eng, body, pieces, ring):
    for first, count in pieces:
        looped = count // ring * ring if count >= 2 * ring else 0
        if looped:
            with eng.Fori(0, looped // ring) as i:
                for u in range(ring):
                    s = first + u
                    body(i * ring + s, s % ring, i + s // ring)
        for s in range(first + looped, first + count):
            body(s, s % ring, s // ring)


def gnn_program(nc, x, src, dst, edge_attr, w_full1, b_full1, w_full2, b_full2,
                w_n1, b_n1, w_n2, b_n2, gamma_int, beta_int, gamma_bn, beta_bn, out):
    N, F = x.shape
    E = edge_attr.shape[0]
    KC = 3 * F // P
    MC = F // P
    TG = 4
    GE = TG * P
    G = E // GE
    REST = E - G * GE
    TAIL = [min(P, REST - t * P) for t in range((REST + P - 1) // P)]
    assert 0 < REST and len(TAIL) == 2
    NT = (E + P - 1) // P
    DUMP = GE
    TR = (N + DUMP + 1023) // 1024 * 1024
    ZR = TR // (G + 1) // P
    assert ZR * P * (G + 1) == TR

    RJ = 5
    NJ = N // P
    C = NJ // RJ
    assert C * RJ == NJ
    NTAIL = N - NJ * P
    NMAIN = NJ * P
    RES = 24

    HM = MC * GE + TG * F
    hm_dram = nc.dram_tensor("hm_dram", (G + 1, P, HM), F32, kind="Internal").ap()
    table = nc.dram_tensor("node_table", (TR, F), F32, kind="Internal").ap()

    w1 = [w_full1, w_n1]
    w2 = [w_full2, w_n2]
    b1 = [b_full1, b_n1]
    b2 = [b_full2, b_n2]
    H, M = 0, 1

    ctx = ExitStack()

    def sem(name):
        return ctx.enter_context(nc.semaphore(name))

    def rows_of(g):
        return [P] * TG if not (isinstance(g, int) and g == G) else TAIL

    with ctx:
        def keep(name, shape, dt=F32):
            return ctx.enter_context(nc.sbuf_tensor(name, shape, dt))

        bank = ctx.enter_context(nc.psum_tensor("bank", [P, 8, 512], F32))
        ident = keep("ident", [P, P])
        ones = keep("ones", [P, P])
        dst_col = keep("dst_col", [P, (G + 1) * TG])
        scatter_idx = keep("scatter_idx", [P, (G + 1) * TG], I32)
        earlier = keep("earlier", [P, (G + 1) * TG])
        ones_r = keep("ones_r", [P, P], F32R)
        h_scale, h_shift = keep("h_scale", [P, MC]), keep("h_shift", [P, MC])
        n_scale, n_shift = keep("n_scale", [P, F]), keep("n_shift", [P, F])
        gamma_row, beta_row = keep("gamma_row", [P, F]), keep("beta_row", [P, F])

        passed = {n: sem("passed_" + n) for n in ("sp", "act", "dve", "pool")}

        def pass_waits(eng, n):
            eng.sem_inc(passed[n], 1)

        def bn_coefficients(dve, mean, var, gamma, beta, scale, shift, step, var_done, std_done):
            n = [0]

            def link(ins):
                n[0] += 1
                ins.then_inc(step, 1)
                dve.wait_ge(step, n[0])
            dve.tensor_scalar(var, var, 0.0, EPS, ALU.max, ALU.add).then_inc(var_done, 1)
            dve.wait_ge(std_done, 1)
            link(dve.reciprocal(var, var))
            link(dve.tensor_tensor(scale, var, gamma, ALU.mult))
            link(dve.tensor_tensor(mean, mean, scale, ALU.mult))
            link(dve.tensor_tensor(shift, beta, mean, ALU.subtract))

        def bn_std(act, var, var_done, std_done):
            act.wait_ge(var_done, 1)
            act.activation(var, var, ACT.Sqrt).then_inc(std_done, 1)

        with ExitStack() as s1:
            def sb(name, shape, dt=F32):
                return s1.enter_context(nc.sbuf_tensor(name, shape, dt))
            w1hl = [sb("w1_hi", [P, 2, KC, F], F32R), sb("w1_lo", [P, 2, KC, F], F32R)]
            w2hl = [sb("w2_hi", [P, 2, MC, F], F32R), sb("w2_lo", [P, 2, MC, F], F32R)]
            xT = [sb("xT_hi", [P, KC, GE], F32R), sb("xT_lo", [P, KC, GE], F32R)]
            g_hl = [sb("g_hi", [P, 2, MC, GE], F32R), sb("g_lo", [P, 2, MC, GE], F32R)]
            w1_raw = sb("w1_raw", [P, 2, MC, 3 * F])
            w2_raw = sb("w2_raw", [P, 2, MC, F])
            land = sb("land", [P, 2, 3, TG, F])
            g32 = sb("g32", [P, 2, GE])
            hm = sb("hm", [P, 2, HM])
            h_stats = sb("h_stats", [P, MC, (G + 1) * 6])
            h_mv = sb("h_mv", [P, MC, 2])
            b1c = sb("b1c", [P, 2, MC])
            b2c = sb("b2c", [P, MC])
            b2b = sb("b2b", [P, F])
            gamma_c, beta_c = sb("gamma_c", [P, MC]), sb("beta_c", [P, MC])
            drow = sb("drow", [P, 2, GE], I32)
            before = sb("before", [P, GE])
            scratch = sb("scratch", [P, 10 * P])
            zero = sb("zero", [P, F])
            idx_raw = sb("idx_raw", [P, 2, P], I32)
            idx_f = sb("idx_f", [P, 2, P])
            idx = sb("idx", [P, 2, (G + 1) * TG], I32)
            cur = sb("cur", [P, 2, 2, TG], I32)
            lane = sb("lane", [P, G + 1, TG], I32)
            lane_f = sb("lane_f", [P, (G + 1) * TG])
            dup = sb("dup", [P, (G + 1) * TG])

            c_ident, c_ones, c_mask = sem("c_ident"), sem("c_ones"), sem("c_mask")
            c_zero, c_idx = sem("c_zero"), sem("c_idx")
            idx_in, w_in, vec_in = sem("idx_in"), sem("w_in"), sem("vec_in")
            idx_float, idx_turned, idx_ready = sem("idx_float"), sem("idx_turned"), sem("idx_ready")
            w_turned, w_hi, w_lo = sem("w_turned"), sem("w_hi"), sem("w_lo")
            cur_ready = sem("cur_ready")
            land_x = [sem("land_x0"), sem("land_x1")]
            land_e = [sem("land_e0"), sem("land_e1")]
            drow_in = [sem("drow_in0"), sem("drow_in1")]
            turned, hi_ready, lo_ready = sem("turned"), sem("hi_ready"), sem("lo_ready")
            l1h_done, l1n_step = sem("l1h_done"), sem("l1n_step")
            silu_done, ghi_ready, glo_ready = sem("silu_done"), sem("ghi_ready"), sem("glo_ready")
            l2_done = [sem("l2h_done"), sem("l2n_done")]
            taken = [sem("h_taken"), sem("m_taken")]
            h_counted = sem("h_counted")
            stored = [sem("hm_stored0"), sem("hm_stored1")]
            counted, zeroed = sem("counted"), sem("zeroed")
            stats_done, bn1, idx_step = sem("stats_done"), sem("bn1"), sem("idx_step")
            bn1_var, bn1_std = sem("bn1_var"), sem("bn1_std")
            lane_made = sem("lane_made")

            bank_of = [[0, 1], [2, 3]]
            TURN, L2 = 4, 6
            units = [(1, b, k) for b in range(2) for k in range(KC)] + \
                    [(2, b, k) for b in range(2) for k in range(MC)]

            def edge_rows(g, t0, rows):
                return edge_attr[bass.ds(g * GE + t0 * P, rows), :]

            block = s1.enter_context(nc.Block())

            @block.sync
            def _(sp):
                sp.wait_ge(c_idx, 1)
                last = (NT - 1) * P
                for i, v in enumerate((dst, src)):
                    sp.dma_start(idx_raw[0:NT - 1, i, :], v[0:last].rearrange("(t p) -> t p", p=P)).then_inc(idx_in, 16)
                    sp.dma_start(idx_raw[NT - 1:NT, i, 0:E - last],
                                 v[last:E].rearrange("(o p) -> o p", o=1)).then_inc(idx_in, 16)

                def load_rows(g, slot):
                    rows = rows_of(g)
                    if len(rows) == TG:
                        sp.dma_start(land[:, slot, 2, :, :],
                                     edge_rows(g, 0, GE).rearrange("(t p) f -> p t f", p=P)).then_inc(land_e[slot], 16)
                        sp.dma_start(drow[:, slot, :], dst[bass.ds(g * GE, GE)].rearrange("(o n) -> o n", o=1)
                                     .to_broadcast([P, GE])).then_inc(drow_in[slot], 16)
                    else:
                        for t, r in enumerate(rows):
                            sp.dma_start(land[0:r, slot, 2, t, :], edge_rows(g, t, r)).then_inc(land_e[slot], 16)
                        sp.dma_start(drow[:, slot, 0:REST], dst[G * GE:E].rearrange("(o n) -> o n", o=1)
                                     .to_broadcast([P, REST])).then_inc(drow_in[slot], 16)

                for b in range(2):
                    sp.dma_start(w1_raw[:, b, :, :], w1[b].rearrange("(c m) k -> m c k", m=P)).then_inc(w_in, 16)
                load_rows(0, 0)
                for b in range(2):
                    sp.dma_start(w2_raw[:, b, :, :], w2[b].rearrange("(c m) k -> m c k", m=P)).then_inc(w_in, 16)
                    sp.dma_start(b1c[:, b, :], b1[b].rearrange("(c m) -> m c", m=P), allow_slow_non_contiguous=True).then_inc(vec_in, 16)
                for to, v in ((b2c, b2[H]), (gamma_c, gamma_int), (beta_c, beta_int)):
                    sp.dma_start(to[:, :], v.rearrange("(c m) -> m c", m=P), allow_slow_non_contiguous=True).then_inc(vec_in, 16)
                for to, v in ((b2b, b2[M]), (gamma_row, gamma_bn), (beta_row, beta_bn)):
                    sp.dma_start(to[:, :], v.rearrange("(o f) -> o f", o=1).to_broadcast([P, F])).then_inc(vec_in, 16)
                load_rows(1, 1)
                sp.wait_ge(c_zero, 1)

                def store(g, slot):
                    sp.wait_ge(taken[H], g * 2 + 2)
                    pass_waits(sp, "sp")
                    sp.wait_ge(taken[M], g * 2 + 2)
                    pass_waits(sp, "sp")
                    sp.dma_start(hm_dram[bass.ds(g, 1), :, :].rearrange("o p n -> (o p) n"),
                                 hm[:, slot, :]).then_inc(stored[slot], 16)

                def body(g, slot, turn):
                    sp.dma_start(table[bass.ds(g * (P * ZR), P * ZR), :].rearrange("(p j) f -> p j f", p=P),
                                 zero[:, :].unsqueeze(1).to_broadcast([P, ZR, F])).then_inc(zeroed, 16)
                    if not (isinstance(g, int) and g == 0):
                        store(g - 1, 1 - slot)
                    if not (isinstance(g, int) and g + 2 > G):
                        sp.wait_ge(turned, KC * g + KC)
                        pass_waits(sp, "sp")
                        sp.wait_ge(counted, g + 1)
                        pass_waits(sp, "sp")
                        load_rows(g + 2, slot)

                in_order(sp, body, [(0, 1), (1, G - 4), (G - 3, 1), (G - 2, 3)], 2)
                sp.wait_ge(taken[H], 2 * G + 2)
                sp.dma_start(hm_dram[G, :, 0:MC * GE].rearrange("p (c e) -> p c e", c=MC)[:, :, 0:REST],
                             hm[:, G % 2, 0:MC * GE].rearrange("p (c e) -> p c e", c=MC)[:, :, 0:REST]).then_inc(stored[G % 2], 16)
                sp.wait_ge(taken[M], 2 * G + 1)
                for t, r in enumerate(TAIL):
                    at = MC * GE + t * F
                    sp.dma_start(hm_dram[G, 0:r, at:at + F], hm[0:r, G % 2, at:at + F]).then_inc(stored[G % 2], 16)
                sp.wait_ge(zeroed, 16 * (G + 1))
                sp.wait_ge(stored[G % 2], 16 * ((G + 1) // 2 + 1 + len(TAIL)))
                sp.wait_ge(stored[1 - G % 2], 16 * (G // 2))

            @block.gpsimd
            def _(pool):
                pool.memset(idx_raw[:, :, :], 0).then_inc(c_idx, 1)
                pool.memset(ident[:, :], 0.0).then_inc(c_ident, 1)
                pool.wait_ge(c_ident, 1)
                pool.affine_select(out=ident[:, :], in_=ident[:, :], compare_op=ALU.not_equal, fill=1.0, base=0,
                                   pattern=[[-1, P]], channel_multiplier=1).then_inc(c_ident, 1)
                pool.memset(zero[:, :], 0.0).then_inc(c_zero, 1)
                pool.memset(ones[:, :], 1.0).then_inc(c_ones, 1)
                pool.memset(ones_r[:, :].bitcast(F32), 1.0).then_inc(c_ones, 1)

                def gather(g, slot):
                    n = len(rows_of(g))
                    pool.tensor_copy(cur[:, slot, :, 0:n], idx[:, :, bass.ds(g * TG, n)]).then_inc(cur_ready, 1)
                    pool.wait_ge(cur_ready, g + 1)
                    pass_waits(pool, "pool")
                    for kind in range(2):
                        for t, r in enumerate(rows_of(g)):
                            pool.indirect_dma_start(
                                out=land[0:r, slot, kind, t, :], out_offset=None, in_=x,
                                in_offset=bass.IndirectOffsetOnAxis(ap=cur[0:r, slot, kind, t:t + 1], axis=0)
                            ).then_inc(land_x[slot], 16)

                pool.wait_ge(idx_ready, 3)
                gather(0, 0)
                gather(1, 1)
                pool.memset(before[:, :], 1.0).then_inc(c_mask, 1)
                pool.wait_ge(c_mask, 1)
                pool.affine_select(out=before[:, GE - P:GE], in_=before[:, GE - P:GE], compare_op=ALU.is_gt, fill=0.0,
                                   base=0, pattern=[[-1, P]], channel_multiplier=1).then_inc(c_mask, 1)
                pool.iota(lane[:, :, :], pattern=[[0, G + 1], [P, TG]], base=N, channel_multiplier=1).then_inc(lane_made, 1)

                def body(g, slot, turn):
                    if not (isinstance(g, int) and g + 2 > G):
                        pool.wait_ge(turned, KC * g + KC)
                        gather(g + 2, slot)

                in_order(pool, body, [(0, 1), (1, G - 4), (G - 3, 2)], 2)

            @block.scalar
            def _(act):
                for u, (layer, b, k) in enumerate(units):
                    act.wait_ge(w_turned, u + 1)
                    to = (w1hl if layer == 1 else w2hl)[0][:, b, k, :]
                    act.activation(to, bank[:, TURN + u % 2, 0:F], ACT.Copy).then_inc(w_hi, 1)
                act.wait_ge(vec_in, 16 * 8)

                def round_chunk(g, k):
                    n = GE if len(rows_of(g)) == TG else REST
                    act.wait_ge(turned, KC * g + k + 1)
                    if not (isinstance(g, int) and g == 0):
                        act.wait_ge(l1n_step, KC * g + (k + 1 - KC))
                    act.activation(xT[0][:, k, 0:n], bank[:, TURN + k % 2, 0:n], ACT.Copy).then_inc(hi_ready, 1)

                def silu(g, b):
                    n = GE if len(rows_of(g)) == TG else REST
                    if b == H:
                        act.wait_ge(l1h_done, g + 1)
                    else:
                        act.wait_ge(l1n_step, KC * g + KC)
                    for c in range(MC):
                        if not (isinstance(g, int) and g == 0 and b == H):
                            act.wait_ge(glo_ready, 4 * g + 2 * b + c - 1)
                        act.activation(g32[:, c, 0:n], bank[:, bank_of[b][c], 0:n], ACT.Silu,
                                       bias=b1c[:, b, c:c + 1]).then_inc(silu_done, 1)

                def take_h(g, slot, turn):
                    n = GE if len(rows_of(g)) == TG else REST
                    if not (isinstance(g, int) and g < 2):
                        act.wait_ge(h_counted, g - 1)
                        act.wait_ge(stored[slot], turn * 16)
                    for c in range(MC):
                        act.wait_ge(l2_done[H], g * 2 + c + 1)
                        act.activation(hm[:, slot, c * GE:c * GE + n], bank[:, L2 + c, 0:n], ACT.Identity,
                                       bias=b2c[:, c:c + 1]).then_inc(taken[H], 1)

                def body(g, slot, turn):
                    silu(g, H)
                    if not (isinstance(g, int) and g == G):
                        for k in range(KC):
                            round_chunk(g + 1, k)
                    silu(g, M)
                    take_h(g, slot, turn)

                for k in range(KC):
                    round_chunk(0, k)
                in_order(act, body, [(0, 1), (1, G - 2), (G - 1, 2)], 2)
                bn_std(act, h_mv[:, :, 1], bn1_var, bn1_std)

            @block.vector
            def _(dve):
                dve.wait_ge(idx_in, 64)
                dve.tensor_copy(idx_f[:, :, :], idx_raw[:, :, :]).then_inc(idx_float, 1)
                dve.wait_ge(idx_turned, 1)
                for i in range(2):
                    dve.tensor_copy(idx[:, i, 0:NT], bank[:, 0, i * P:i * P + NT]).then_inc(idx_ready, 1)
                dve.tensor_copy(dst_col[:, 0:NT], bank[:, 0, 0:NT]).then_inc(idx_ready, 1)
                dve.memset(earlier[:, :], 0.0).then_inc(idx_ready, 1)
                for u, (layer, b, k) in enumerate(units):
                    dve.wait_ge(w_hi, u + 1)
                    hl = w1hl if layer == 1 else w2hl
                    dve.tensor_tensor(hl[1][:, b, k, :], bank[:, TURN + u % 2, 0:F],
                                      hl[0][:, b, k, :].bitcast(F32), ALU.subtract).then_inc(w_lo, 1)
                dve.wait_ge(vec_in, 16 * 8)

                def rest_chunk(g, k):
                    n = GE if len(rows_of(g)) == TG else REST
                    dve.wait_ge(hi_ready, KC * g + k + 1)
                    dve.tensor_tensor(xT[1][:, k, 0:n], bank[:, TURN + k % 2, 0:n],
                                      xT[0][:, k, 0:n].bitcast(F32), ALU.subtract).then_inc(lo_ready, 1)

                def split(g, b):
                    n = GE if len(rows_of(g)) == TG else REST
                    if not (isinstance(g, int) and g == 0):
                        dve.wait_ge(l2_done[b], g * 2)
                    for c in range(MC):
                        dve.wait_ge(silu_done, 4 * g + 2 * b + c + 1)
                        dve.tensor_copy(g_hl[0][:, b, c, 0:n], g32[:, c, 0:n]).then_inc(ghi_ready, 1)
                    for c in range(MC):
                        dve.wait_ge(ghi_ready, 4 * g + 2 * b + c + 1)
                        dve.tensor_tensor(g_hl[1][:, b, c, 0:n], g32[:, c, 0:n],
                                          g_hl[0][:, b, c, 0:n].bitcast(F32), ALU.subtract).then_inc(glo_ready, 1)

                def take_m(g, slot):
                    rows = rows_of(g)
                    if len(rows) == TG:
                        for q in range(2):
                            dve.wait_ge(l2_done[M], g * 2 + q + 1)
                            at = MC * GE + 2 * q * F
                            dve.tensor_tensor(hm[:, slot, at:at + 2 * F].rearrange("p (t f) -> p t f", t=2),
                                              bank[:, L2 + q, :].rearrange("p (t f) -> p t f", t=2),
                                              b2b[:, :].unsqueeze(1).to_broadcast([P, 2, F]), ALU.add).then_inc(taken[M], 1)
                    else:
                        dve.wait_ge(l2_done[M], g * 2 + 1)
                        for t, r in enumerate(rows):
                            at = MC * GE + t * F
                            last = dve.tensor_tensor(hm[0:r, slot, at:at + F], bank[0:r, L2, t * F:(t + 1) * F],
                                                     b2b[0:r, :], ALU.add)
                        last.then_inc(taken[M], 1)

                def count_h(g, slot):
                    n = GE if len(rows_of(g)) == TG else REST
                    dve.wait_ge(taken[H], g * 2 + 2)
                    pass_waits(dve, "dve")
                    for c in range(MC):
                        last = dve.bn_stats(h_stats[:, c, bass.ds(g * 6, 6)], hm[:, slot, c * GE:c * GE + n])
                    last.then_inc(h_counted, 1)

                def count_earlier(g, slot, turn):
                    rows = rows_of(g)
                    dve.wait_ge(drow_in[slot], turn * 16 + 16)
                    if not (isinstance(g, int) and g == 0):
                        dve.wait_ge(counted, g)
                    at = 0
                    for a, r in enumerate(rows):
                        n = min((a + 1) * P, GE if len(rows) == TG else REST)
                        last = dve.scalar_tensor_tensor(
                            out=scratch[0:r, at:at + n], in0=drow[0:r, slot, 0:n],
                            scalar=dst_col[0:r, bass.ds(g * TG + a, 1)], in1=before[0:r, GE - P - a * P:GE - P - a * P + n],
                            op0=ALU.is_equal, op1=ALU.mult, accum_out=earlier[0:r, bass.ds(g * TG + a, 1)])
                        at += n
                    last.then_inc(counted, 1)

                def body(g, slot, turn):
                    split(g, H)
                    if not (isinstance(g, int) and g == 0):
                        take_m(g - 1, 1 - slot)
                        count_h(g - 1, 1 - slot)
                    if not (isinstance(g, int) and g == G):
                        for k in range(KC):
                            rest_chunk(g + 1, k)
                    split(g, M)
                    count_earlier(g, slot, turn)

                for k in range(KC):
                    rest_chunk(0, k)
                dve.wait_ge(c_mask, 2)
                dve.wait_ge(idx_ready, 4)
                in_order(dve, body, [(0, 1), (1, G - 2), (G - 1, 2)], 2)
                count_h(G, G % 2)
                take_m(G, G % 2)
                dve.wait_ge(lane_made, 1)
                dve.wait_ge(counted, G + 1)
                steps = [
                    lambda: dve.tensor_copy(lane_f[:, :], lane[:, :, :].rearrange("p g t -> p (g t)")),
                    lambda: dve.tensor_scalar(dup[:, :], earlier[:, :], 0.0, None, ALU.is_gt),
                    lambda: dve.tensor_tensor(lane_f[:, 0:NT], lane_f[:, 0:NT], dst_col[:, 0:NT], ALU.subtract),
                    lambda: dve.tensor_tensor(lane_f[:, 0:NT], lane_f[:, 0:NT], dup[:, 0:NT], ALU.mult),
                    lambda: dve.tensor_tensor(scatter_idx[:, 0:NT], lane_f[:, 0:NT], dst_col[:, 0:NT], ALU.add),
                ]
                for i, s in enumerate(steps):
                    s().then_inc(idx_step, 1)
                    dve.wait_ge(idx_step, i + 1)
                dve.wait_ge(h_counted, G + 1)
                for c in range(MC):
                    last = dve.bn_aggr(h_mv[:, c, :], h_stats[:, c, :])
                last.then_inc(stats_done, 1)
                dve.wait_ge(stats_done, 1)
                bn_coefficients(dve, h_mv[:, :, 0], h_mv[:, :, 1], gamma_c[:, :], beta_c[:, :], h_scale[:, :], h_shift[:, :],
                                bn1, bn1_var, bn1_std)

            @block.tensor
            def _(pe):
                pe.wait_ge(idx_float, 1)
                pe.wait_ge(c_ident, 2)
                for i in range(2):
                    last = pe.transpose(bank[:, 0, i * P:i * P + NT], idx_f[0:NT, i, :], ident[0:NT, 0:NT])
                last.then_inc(idx_turned, 1)
                pe.wait_ge(w_in, 64)
                for u, (layer, b, k) in enumerate(units):
                    if u >= 2:
                        pe.wait_ge(w_lo, u - 1)
                    for c in range(MC):
                        raw = (w1_raw if layer == 1 else w2_raw)[:, b, c, k * P:(k + 1) * P]
                        last = pe.transpose(bank[:, TURN + u % 2, c * P:(c + 1) * P], raw, ident[:, :])
                    last.then_inc(w_turned, 1)

                def turn_chunk(g, k, slot, turn):
                    rows = rows_of(g)
                    n_in = 8 if len(rows) == TG else 2 * len(rows)
                    if k == 0:
                        pe.wait_ge(land_x[slot], turn * 128 + 16 * n_in)
                    if k == 2 * F // P:
                        pe.wait_ge(land_e[slot], turn * 16 + (16 if len(rows) == TG else 32))
                    if not (isinstance(g, int) and g == 0 and k < 2):
                        pe.wait_ge(lo_ready, KC * g + k - 1)
                    kind, half = divmod(k, F // P)
                    for t, r in enumerate(rows):
                        last = pe.transpose(bank[:, TURN + k % 2, t * P:t * P + r],
                                            land[0:r, slot, kind, t, half * P:(half + 1) * P], ident[0:r, 0:r])
                    last.then_inc(turned, 1)

                def layer1(g, b, k):
                    n = GE if len(rows_of(g)) == TG else REST
                    if k == 0 and not (isinstance(g, int) and g == 0):
                        pe.wait_ge(silu_done, 4 * g + (2 * b - 2))
                    if b == H:
                        pe.wait_ge(lo_ready, KC * g + k + 1)
                    for c in range(MC):
                        for j, (w, v) in enumerate(((0, 0), (0, 1), (1, 0))):
                            last = pe.matmul(bank[:, bank_of[b][c], 0:n], w1hl[w][:, b, k, c * P:(c + 1) * P],
                                             xT[v][:, k, 0:n], start=(k == 0 and j == 0), stop=(k == KC - 1 and j == 2))
                    if b == M:
                        last.then_inc(l1n_step, 1)
                    elif k == KC - 1:
                        last.then_inc(l1h_done, 1)

                def layer2_h(g):
                    n = GE if len(rows_of(g)) == TG else REST
                    pe.wait_ge(glo_ready, 4 * g + 2)
                    for c in range(MC):
                        if not (isinstance(g, int) and g == 0):
                            pe.wait_ge(taken[M], g * 2 - 1 + c)
                        i = 0
                        for k in range(MC):
                            for w, v in ((0, 0), (0, 1), (1, 0)):
                                last = pe.matmul(bank[:, L2 + c, 0:n], w2hl[w][:, H, k, c * P:(c + 1) * P],
                                                 g_hl[v][:, H, k, 0:n], start=(i == 0), stop=(i == 3 * MC - 1))
                                i += 1
                        last.then_inc(l2_done[H], 1)

                def layer2_m(g):
                    rows = rows_of(g)
                    pe.wait_ge(glo_ready, 4 * g + 4)
                    for t, r in enumerate(rows):
                        if t % 2 == 0:
                            pe.wait_ge(taken[H], g * 2 + (1 + t // 2 if len(rows) == TG else 1))
                        i = 0
                        for k in range(MC):
                            for v, w in ((0, 0), (0, 1), (1, 0)):
                                last = pe.matmul(bank[0:r, L2 + t // 2, (t % 2) * F:(t % 2 + 1) * F],
                                                 g_hl[v][:, M, k, t * P:t * P + r], w2hl[w][:, M, k, :],
                                                 start=(i == 0), stop=(i == 3 * MC - 1))
                                i += 1
                        if t % 2 == 1:
                            last.then_inc(l2_done[M], 1)

                def body(g, slot, turn):
                    for k in range(KC):
                        layer1(g, H, k)
                    if not (isinstance(g, int) and g == 0):
                        layer2_m(g - 1)
                    for k in range(KC):
                        layer1(g, M, k)
                        if not (isinstance(g, int) and g == G):
                            turn_chunk(g + 1, k, 1 - slot, turn + slot)
                    layer2_h(g)

                pe.wait_ge(w_lo, len(units))
                for k in range(KC):
                    turn_chunk(0, k, 0, 0)
                in_order(pe, body, [(0, 1), (1, G - 2), (G - 1, 2)], 2)
                layer2_m(G)

        with ExitStack() as s2:
            def sb(name, shape, dt=F32):
                return s2.enter_context(nc.sbuf_tensor(name, shape, dt))
            R2 = 4
            hm2 = sb("hm2", [P, R2, HM])
            drow2 = sb("drow2", [P, R2, GE], I32)
            score = sb("score", [P, 2, MC, GE])
            msg = sb("msg", [P, 2, TG, F])
            msg_hl = [sb("msg_hi", [P, 2, TG, F], F32R), sb("msg_lo", [P, 2, TG, F], F32R)]
            same = sb("same", [P, 2, 10 * P], F32R)
            sums = sb("sums", [P, 2, TG, F])
            cur2 = sb("cur2", [P, 2, TG], I32)
            group_in = [sem(f"group_in{i}") for i in range(R2)]
            scored, score_turned, msg_ready = sem("scored"), sem("score_turned"), sem("msg_ready")
            msg_hi_ready, msg_lo_ready, same_ready = sem("msg_hi_ready"), sem("msg_lo_ready"), sem("same_ready")
            combined, sums_ready, added = sem("combined"), sem("sums_ready"), sem("added")
            cur2_ready = sem("cur2_ready")
            same_at = [sum(range(b + 1)) * P for b in range(TG)]
            block = s2.enter_context(nc.Block())

            def is_first(g, n=1):
                return isinstance(g, int) and g < n

            def parts_of(g):
                rows = rows_of(g)
                return [(P, slice(0, TG))] if len(rows) == TG else [(r, slice(t, t + 1)) for t, r in enumerate(rows)]

            def edge_banks(first, par):
                return bank[:, first + 2 * par:first + 2 * par + 2, :].rearrange("p b (t f) -> p (b t) f", t=2)

            @block.sync
            def _(sp):
                def load(g, slot):
                    rows = rows_of(g)
                    if len(rows) == TG:
                        sp.dma_start(hm2[:, slot, :],
                                     hm_dram[bass.ds(g, 1), :, :].rearrange("o p n -> (o p) n")).then_inc(group_in[slot], 16)
                        sp.dma_start(drow2[:, slot, :], dst[bass.ds(g * GE, GE)].rearrange("(o n) -> o n", o=1)
                                     .to_broadcast([P, GE])).then_inc(group_in[slot], 16)
                    else:
                        sp.dma_start(hm2[:, slot, 0:MC * GE].rearrange("p (c e) -> p c e", c=MC)[:, :, 0:REST],
                                     hm_dram[G, :, 0:MC * GE].rearrange("p (c e) -> p c e", c=MC)[:, :, 0:REST]).then_inc(group_in[slot], 16)
                        for t, r in enumerate(rows):
                            at = MC * GE + t * F
                            sp.dma_start(hm2[0:r, slot, at:at + F], hm_dram[G, 0:r, at:at + F]).then_inc(group_in[slot], 16)
                        sp.dma_start(drow2[:, slot, 0:REST], dst[G * GE:E].rearrange("(o n) -> o n", o=1)
                                     .to_broadcast([P, REST])).then_inc(group_in[slot], 16)

                for g in range(R2):
                    load(g, g)

                def body(g, slot, turn):
                    sp.wait_ge(same_ready, g + 1)
                    pass_waits(sp, "sp")
                    load(g + R2, slot)
                in_order(sp, body, [(0, G - R2), (G - R2, 1)], R2)

            SC, CS = 4, 6

            @block.vector
            def _(dve):
                def message(g, slot, turn):
                    par = slot % 2
                    if not is_first(g, 2):
                        dve.wait_ge(msg_lo_ready, g - 1)
                    dve.wait_ge(score_turned, g + 1)
                    for r, ts in parts_of(g):
                        k = TG if r == P and ts.stop == TG else 1
                        m = hm2[0:r, slot, MC * GE:HM].rearrange("p (t f) -> p t f", f=F)[:, ts, :]
                        last = dve.tensor_tensor(msg[0:r, par, ts, :], edge_banks(SC, 0)[0:r, ts, :], m, ALU.mult)
                    last.then_inc(msg_ready, 1)

                def compare(g, slot):
                    rows = rows_of(g)
                    if not is_first(g, 2):
                        dve.wait_ge(combined, g - 1)
                    for b, r in enumerate(rows):
                        n = min((b + 1) * P, GE if len(rows) == TG else REST)
                        last = dve.tensor_scalar(same[0:r, slot % 2, same_at[b]:same_at[b] + n], drow2[0:r, slot, 0:n],
                                                 dst_col[0:r, bass.ds(g * TG + b, 1)], None, ALU.is_equal)
                    last.then_inc(same_ready, 1)

                def low(g, slot):
                    par = slot % 2
                    dve.wait_ge(msg_hi_ready, g + 1)
                    for r, ts in parts_of(g):
                        last = dve.tensor_tensor(msg_hl[1][0:r, par, ts, :], msg[0:r, par, ts, :],
                                                 msg_hl[0][0:r, par, ts, :].bitcast(F32), ALU.subtract)
                    last.then_inc(msg_lo_ready, 1)

                def body(g, slot, turn):
                    low(g, slot)
                    if not (isinstance(g, int) and g == G):
                        message(g + 1, (slot + 1) % R2, turn + (slot + 1) // R2)
                        compare(g + 1, (slot + 1) % R2)
                message(0, 0, 0)
                compare(0, 0)
                in_order(dve, body, [(0, 2), (2, G - 4), (G - 2, 3)], R2)

            @block.scalar
            def _(act):
                def score_of(g, slot, turn):
                    rows = rows_of(g)
                    n = GE if len(rows) == TG else REST
                    act.wait_ge(group_in[slot], turn * 32 + (32 if len(rows) == TG else 64))
                    if not is_first(g, 2):
                        act.wait_ge(score_turned, g - 1)
                    for c in range(MC):
                        last = act.activation(score[:, slot % 2, c, 0:n], hm2[:, slot, c * GE:c * GE + n], ACT.Sigmoid,
                                              bias=h_shift[:, c:c + 1], scale=h_scale[:, c:c + 1])
                    last.then_inc(scored, 1)

                def high(g, slot):
                    par = slot % 2
                    act.wait_ge(msg_ready, g + 1)
                    if not is_first(g, 2):
                        act.wait_ge(combined, g - 1)
                    for r, ts in parts_of(g):
                        last = act.activation(msg_hl[0][0:r, par, ts, :], msg[0:r, par, ts, :], ACT.Copy)
                    last.then_inc(msg_hi_ready, 1)

                def take_sums(g, slot):
                    par = slot % 2
                    act.wait_ge(combined, g + 1)
                    if not is_first(g, 2):
                        act.wait_ge(added, 64 * g - 64)
                    for r, ts in parts_of(g):
                        last = act.activation(sums[0:r, par, ts, :], edge_banks(0, par)[0:r, ts, :], ACT.Copy)
                    last.then_inc(sums_ready, 1)

                def body(g, slot, turn):
                    if not (isinstance(g, int) and g + 1 > G):
                        high(g + 1, slot + 1)
                    if not (isinstance(g, int) and g + 2 > G):
                        score_of(g + 2, (slot + 2) % R2, turn + (slot + 2) // R2)
                    take_sums(g, slot)
                score_of(0, 0, 0)
                score_of(1, 1, 0)
                high(0, 0)
                in_order(act, body, [(0, 2), (2, G - 4), (G - 2, 3)], R2)

            @block.tensor
            def _(pe):
                def turn_scores(g, slot):
                    par = slot % 2
                    pe.wait_ge(scored, g + 1)
                    if not is_first(g, 1):
                        pe.wait_ge(msg_ready, g)
                    for c in range(MC):
                        for t, r in enumerate(rows_of(g)):
                            last = pe.transpose(edge_banks(SC, 0)[0:r, t, c * P:(c + 1) * P],
                                                score[:, par, c, t * P:t * P + r], ident[:, :])
                    last.then_inc(score_turned, 1)

                def combine(g, slot):
                    rows, par = rows_of(g), slot % 2
                    pe.wait_ge(same_ready, g + 1)
                    pe.wait_ge(msg_lo_ready, g + 1)
                    if not is_first(g, 2):
                        pe.wait_ge(sums_ready, g - 1)
                    for a, ra in enumerate(rows):
                        for b in range(a, len(rows)):
                            for v in range(2):
                                last = pe.matmul(edge_banks(0, par)[0:ra, a, :],
                                                 same[0:rows[b], par, same_at[b] + a * P:same_at[b] + a * P + ra],
                                                 msg_hl[v][0:rows[b], par, b, :],
                                                 start=(b == a and v == 0), stop=(b == len(rows) - 1 and v == 1))
                    for b, r in enumerate(rows):
                        for v in range(2):
                            last = pe.matmul(bank[:, CS, 0:F], ones_r[0:r, :], msg_hl[v][0:r, par, b, :],
                                             start=(is_first(g, 1) and b == 0 and v == 0),
                                             stop=(isinstance(g, int) and g == G and b == len(rows) - 1 and v == 1))
                    last.then_inc(combined, 1)

                def body(g, slot, turn):
                    if not (isinstance(g, int) and g + 1 > G):
                        turn_scores(g + 1, 1 - slot)
                    combine(g, slot)
                turn_scores(0, 0)
                in_order(pe, body, [(0, 2), (2, G - 4), (G - 2, 3)], 2)

            @block.gpsimd
            def _(pool):
                def body(g, slot, turn):
                    rows = rows_of(g)
                    pool.tensor_copy(cur2[:, slot, 0:len(rows)], scatter_idx[:, bass.ds(g * TG, len(rows))]).then_inc(cur2_ready, 1)
                    pool.wait_ge(cur2_ready, g + 1)
                    pass_waits(pool, "pool")
                    pool.wait_ge(sums_ready, g + 1)
                    pass_waits(pool, "pool")
                    if not is_first(g, 1):
                        pool.wait_ge(added, 64 * g)
                        pass_waits(pool, "pool")
                    for t, r in enumerate(rows):
                        pool.indirect_dma_start(
                            out=table, out_offset=bass.IndirectOffsetOnAxis(ap=cur2[0:r, slot, t:t + 1], axis=0),
                            in_=sums[0:r, slot, t, :], in_offset=None, compute_op=ALU.add).then_inc(added, 16)
                in_order(pool, body, [(0, 1), (1, G - 2), (G - 1, 2)], 2)
                pool.wait_ge(added, 64 * G + 16 * len(TAIL))

        with ExitStack() as s3:
            def sb(name, shape, dt=F32):
                return s3.enter_context(nc.sbuf_tensor(name, shape, dt))
            R = 3
            RT = 2 * R
            W = RJ * F
            assert RES % RT == 0
            res = sb("res", [P, RES, W])
            tr = sb("tr", [P, RT, W])
            xr = sb("xr", [P, R, W])
            ob = sb("ob", [P, R, W])
            unread = sb("unread", [P, W], mybir.dt.bfloat16)
            tail_t = sb("tail_t", [P, F])
            tail_x = sb("tail_x", [P, F])
            tail_o = sb("tail_o", [P, F])
            row_sum = sb("row_sum", [P, RT, RJ])
            row_sq = sb("row_sq", [P, RT, RJ])
            row_mean = sb("row_mean", [P, RT, RJ])
            row_var = sb("row_var", [P, RT, RJ])
            row_rstd = sb("row_rstd", [P, RT, RJ])
            row_shift = sb("row_shift", [P, RT, RJ])

            table_v = table[0:NMAIN, :].rearrange("(p c j) f -> p c (j f)", p=P, c=C)
            x_v = x[0:NMAIN, :].rearrange("(p c j) f -> p c (j f)", p=P, c=C)
            out_v = out[0:NMAIN, :].rearrange("(p c j) f -> p c (j f)", p=P, c=C)
            acc2 = sb("acc2", [P, W])
            shift_hl = sb("shift_hl", [64, 2 * F], F32R)
            n_mean, n_var = sb("n_mean", [P, F]), sb("n_var", [P, F])

            def chunk(v, c):
                return v[:, bass.ds(c, 1), :].rearrange("p o n -> p (o n)")

            ahead = (RES - 1 - 3) // RT * RT
            PIECES = [(0, 3), (3, ahead), (3 + ahead, RES - 1 - ahead),
                      (RES + 2, (C - 1 - RES - 2) // RT * RT)]
            PIECES.append((sum(PIECES[-1]), C - sum(PIECES[-1])))
            stays = {}

            def chunks_in_order(eng, body):
                for first, count in PIECES:
                    stays["now"] = first < RES
                    in_order(eng, body, [(first, count)], RT)

            def in_res(c):
                return c < RES if isinstance(c, int) else stays["now"]

            def kept(c, slot, part=slice(0, W)):
                if in_res(c):
                    return res[:, bass.ds(c, 1), part].rearrange("p o n -> p (o n)")
                return tr[:, slot % RT, part]

            def row(j):
                return slice(j * F, (j + 1) * F)

            t_in = [sem(f"t_in{i}") for i in range(RT)]
            tail_in, sq_ready, sq_summed = sem("tail_in"), sem("sq_ready"), sem("sq_summed")
            tail_sq, sq_zero = sem("tail_sq"), sem("sq_zero")
            n_step, shift_ready = sem("n_step"), sem("shift_ready")
            cols_ready, bn2, bn2_var, bn2_std = sem("cols_ready"), sem("bn2"), sem("bn2_var"), sem("bn2_std")

            def sums_sp(sp):
                sp.dma_start(tail_t[0:NTAIL, :], table[NMAIN:N, :]).then_inc(tail_in, 16)
                sp.dma_start(tail_x[0:NTAIL, :], x[NMAIN:N, :]).then_inc(tail_in, 16)

                def body(c, slot, turn):
                    if not is_first(c, RT):
                        sp.wait_ge(sq_ready, c - RT + 1)
                        pass_waits(sp, "sp")
                    sp.dma_start(kept(c, slot), chunk(table_v, c)).then_inc(t_in[slot], 16)
                stays["now"] = True
                in_order(sp, body, [(0, RT), (RT, RES - RT)], RT)
                stays["now"] = False
                in_order(sp, body, [(RES, C - RES)], RT)

            def sums_act(act):
                def body(c, slot, turn):
                    act.wait_ge(t_in[slot], turn * 16 + 16)
                    if not is_first(c, R):
                        act.wait_ge(sq_summed, c - R + 1)
                    pass_waits(act, "act")
                    act.activation(ob[:, slot % R, :], kept(c, slot), ACT.Square).then_inc(sq_ready, 1)
                chunks_in_order(act, body)
                act.wait_ge(tail_in, 32)
                act.activation(tail_o[0:NTAIL, :], tail_t[0:NTAIL, :], ACT.Square).then_inc(tail_sq, 1)
                bn_std(act, n_var[:, :], bn2_var, bn2_std)

            def sums_dve(dve):
                dve.memset(shift_hl[:, :].bitcast(F32), 0.0)
                dve.memset(acc2[:, :], 0.0).then_inc(sq_zero, 1)
                dve.wait_ge(sq_zero, 1)

                def body(c, slot, turn):
                    dve.wait_ge(sq_ready, c + 1)
                    if not is_first(c, 1):
                        dve.wait_ge(sq_summed, c)
                    dve.tensor_tensor(acc2[:, :], acc2[:, :], ob[:, slot % R, :], ALU.add).then_inc(sq_summed, 1)
                chunks_in_order(dve, body)
                dve.wait_ge(cols_ready, 1)
                dve.tensor_scalar(n_mean[:, :], bank[:, CS, 0:F], 1.0 / N, None, ALU.mult).then_inc(n_step, 1)
                dve.wait_ge(n_step, 1)
                dve.tensor_tensor(n_var[:, :], n_mean[:, :], n_mean[:, :], ALU.mult).then_inc(n_step, 1)
                dve.wait_ge(n_step, 2)
                dve.scalar_tensor_tensor(out=n_var[:, :], in0=bank[:, 1, 0:F], scalar=1.0 / N, in1=n_var[:, :],
                                         op0=ALU.mult, op1=ALU.subtract).then_inc(n_step, 1)
                dve.wait_ge(n_step, 3)
                bn_coefficients(dve, n_mean[:, :], n_var[:, :], gamma_row[:, :], beta_row[:, :],
                                n_scale[:, :], n_shift[:, :], bn2, bn2_var, bn2_std)
                for half in range(2):
                    to = slice(half * F, (half + 1) * F)
                    for r in (0, 32):
                        last = dve.tensor_copy(shift_hl[r:r + 1, to], n_shift[r:r + 1, :])
                last.then_inc(n_step, 1)
                dve.wait_ge(n_step, 4)
                for half in range(2):
                    to = slice(half * F, (half + 1) * F)
                    last = dve.tensor_tensor(shift_hl[32:33, to], n_shift[32:33, :],
                                             shift_hl[32:33, to].bitcast(F32), ALU.subtract)
                last.then_inc(shift_ready, 1)

            def sums_pe(pe):
                pe.wait_ge(tail_sq, 1)
                pe.matmul(bank[:, 1, 0:F], ones[0:NTAIL, :], tail_o[0:NTAIL, :], start=True, stop=False)
                pe.wait_ge(sq_summed, C)
                for j in range(RJ):
                    last = pe.matmul(bank[:, 1, 0:F], ones[:, :], acc2[:, row(j)], start=False, stop=(j == RJ - 1))
                last.then_inc(cols_ready, 1)

            x_in = [sem(f"x_in{i}") for i in range(R)]
            t_again = [sem(f"t_again{i}") for i in range(RT)]
            t_scaled, z_ready, normed_dve = sem("t_scaled"), sem("z_ready"), sem("normed_dve")
            y_ready, y_squared, small = sem("y_ready"), sem("y_squared"), sem("small")
            var_ready, std_ready, inverse, coef, normed = sem("var_ready"), sem("std_ready"), sem("inverse"), sem("coef"), sem("normed")
            out_done = [sem(f"out_done{i}") for i in range(R)]
            tail_ready, tail_stored, tail_step, tail_std = sem("tail_ready"), sem("tail_stored"), sem("tail_step"), sem("tail_std")
            tail_var = sem("tail_var")
            block = s3.enter_context(nc.Block())
            XB = [0, 3]
            NA = 3

            @block.sync
            def _(sp):
                sums_sp(sp)

                def body(c, slot, turn):
                    if not is_first(c, R):
                        sp.wait_ge(y_ready, c - R + 1)
                        pass_waits(sp, "sp")
                    sp.dma_start(xr[:, slot % R, :], chunk(x_v, c)).then_inc(x_in[slot % R], 16)
                    if not in_res(c):
                        if isinstance(c, int) and c < RES + RT:
                            sp.wait_ge(sq_ready, C)
                        else:
                            sp.wait_ge(normed, c - RT + 1)
                            sp.wait_ge(normed_dve, c - RT + 1)
                        pass_waits(sp, "sp")
                        sp.dma_start(tr[:, slot, :], chunk(table_v, c)).then_inc(t_again[slot], 16)
                chunks_in_order(sp, body)
                sp.wait_ge(tail_ready, 1)
                sp.dma_start(out[NMAIN:N, :], tail_o[0:NTAIL, :]).then_inc(tail_stored, 16)
                sp.wait_ge(tail_stored, 16)
                for i in range(R):
                    sp.wait_ge(out_done[i], 16 * ((C - i + R - 1) // R))

            @block.tensor
            def _(pe):
                sums_pe(pe)
                pe.wait_ge(shift_ready, 1)

                def body(c, slot, turn):
                    pe.wait_ge(x_in[slot % R], turn * 32 + 16 * (slot // R) + 16)
                    if not is_first(c, 2):
                        pe.wait_ge(y_ready, c - 1)
                    for b in range((W + 511) // 512):
                        n = min(512, W - b * 512)
                        o = bank[:, XB[slot % 2] + b, 0:n]
                        pe.matmul(o, ident[:, :], xr[:, slot % R, b * 512:b * 512 + n], start=True, stop=False)
                        pe.matmul(o, ones_r[0:64, :], shift_hl[:, 0:n], start=False, stop=False)
                    pe.wait_ge(t_scaled, c + 1)
                    for b in range((W + 511) // 512):
                        n = min(512, W - b * 512)
                        last = pe.matmul(bank[:, XB[slot % 2] + b, 0:n], ident[:, :], kept(c, slot, slice(b * 512, b * 512 + n)),
                                         start=False, stop=True)
                    last.then_inc(z_ready, 1)
                chunks_in_order(pe, body)

            @block.vector
            def _(dve):
                sums_dve(dve)

                def scale(c, slot, turn):
                    if not in_res(c):
                        dve.wait_ge(t_again[slot], (turn - RES // RT) * 16 + 16)
                    t = kept(c, slot).rearrange("p (j f) -> p j f", f=F)
                    dve.tensor_tensor(t, t, n_scale[:, :].unsqueeze(1).to_broadcast([P, RJ, F]), ALU.mult).then_inc(t_scaled, 1)

                def relu_add(c, slot, between):
                    z = bank[:, XB[slot % 2]:XB[slot % 2] + 3, :].rearrange("p b n -> p (b n)")
                    dve.wait_ge(z_ready, c + 1)
                    for j in range(RJ):
                        last = dve.scalar_tensor_tensor(out=kept(c, slot, row(j)), in0=z[:, row(j)], scalar=0.0,
                                                        in1=xr[:, slot % R, row(j)],
                                                        op0=ALU.max, op1=ALU.add, accum_out=row_sum[:, slot, j:j + 1])
                        if j == RJ - 1:
                            last.then_inc(y_ready, 1)
                        elif between:
                            between[j]()

                def variance_steps(c, slot):
                    mean, var = row_mean[:, slot, :], row_var[:, slot, :]

                    def mean_of():
                        dve.wait_ge(y_ready, c + 1)
                        dve.tensor_scalar(mean, row_sum[:, slot, :], 1.0 / F, None, ALU.mult).then_inc(small, 1)

                    def mean_squared():
                        dve.wait_ge(small, 3 * c + 1)
                        dve.tensor_tensor(var, mean, mean, ALU.mult).then_inc(small, 1)

                    def variance():
                        dve.wait_ge(y_squared, c + 1)
                        dve.wait_ge(small, 3 * c + 2)
                        dve.scalar_tensor_tensor(out=var, in0=row_sq[:, slot, :], scalar=1.0 / F, in1=var,
                                                 op0=ALU.mult, op1=ALU.subtract).then_inc(small, 1)

                    def guarded():
                        dve.wait_ge(small, 3 * c + 3)
                        dve.tensor_scalar(var, var, 0.0, EPS, ALU.max, ALU.add).then_inc(var_ready, 1)
                    return [mean_of, mean_squared, variance, guarded]

                def invert(c, slot):
                    dve.wait_ge(std_ready, c + 1)
                    dve.reciprocal(row_rstd[:, slot, :], row_var[:, slot, :]).then_inc(inverse, 1)

                def shift_of(c, slot):
                    dve.wait_ge(inverse, c + 1)
                    dve.scalar_tensor_tensor(out=row_shift[:, slot, :], in0=row_mean[:, slot, :], scalar=-1.0,
                                             in1=row_rstd[:, slot, :], op0=ALU.mult, op1=ALU.mult).then_inc(coef, 1)

                def norm(c, slot, turn):
                    dve.wait_ge(coef, c + 1)
                    if not is_first(c, R):
                        dve.wait_ge(out_done[slot % R], turn * 32 + 16 * (slot // R))
                    pass_waits(dve, "dve")
                    for j in range(NA, RJ):
                        last = dve.tensor_scalar(ob[:, slot % R, row(j)], kept(c, slot, row(j)), row_rstd[:, slot, j:j + 1],
                                                 row_shift[:, slot, j:j + 1], ALU.mult, ALU.add)
                    last.then_inc(normed_dve, 1)

                def body(c, slot, turn):
                    two_back = c - 2, (slot + RT - 2) % RT
                    if not is_first(c, 2):
                        invert(*two_back)
                    if not (isinstance(c, int) and c == C - 1):
                        scale(c + 1, (slot + 1) % RT, turn + (slot + 1) // RT)
                    if not is_first(c, 2):
                        shift_of(*two_back)
                    relu_add(c, slot, [] if is_first(c, 1) else variance_steps(c - 1, (slot + RT - 1) % RT))
                    if not is_first(c, 2):
                        norm(*two_back, turn - (1 if slot < 2 else 0))
                scale(0, 0, 0)
                chunks_in_order(dve, body)
                for step in variance_steps(C - 1, (C - 1) % RT):
                    step()
                for c in (C - 2, C - 1):
                    invert(c, c % RT)
                    shift_of(c, c % RT)
                    norm(c, c % RT, c // RT)
                n = NTAIL
                s = [0]

                def link(ins):
                    s[0] += 1
                    ins.then_inc(tail_step, 1)
                    dve.wait_ge(tail_step, s[0])
                dve.wait_ge(normed, C)
                dve.wait_ge(normed_dve, C)
                total, squares, mean, var, rstd = (v[0:n, 0, 0:1] for v in (row_sum, row_sq, row_mean, row_var, row_rstd))
                tt = tail_t[0:n, :]
                link(dve.tensor_tensor(tt, tt, n_scale[0:n, :], ALU.mult))
                link(dve.tensor_tensor(tt, tt, n_shift[0:n, :], ALU.add))
                link(dve.tensor_tensor(tt, tt, tail_x[0:n, :], ALU.add))
                link(dve.scalar_tensor_tensor(out=tt, in0=tt, scalar=0.0, in1=tail_x[0:n, :],
                                              op0=ALU.max, op1=ALU.add, accum_out=total))
                link(dve.scalar_tensor_tensor(out=tail_o[0:n, :], in0=tt, scalar=1.0, in1=tt,
                                              op0=ALU.mult, op1=ALU.mult, accum_out=squares))
                link(dve.tensor_scalar(mean, total, 1.0 / F, None, ALU.mult))
                link(dve.tensor_tensor(var, mean, mean, ALU.mult))
                link(dve.scalar_tensor_tensor(out=var, in0=squares, scalar=1.0 / F, in1=var, op0=ALU.mult, op1=ALU.subtract))
                dve.tensor_scalar(var, var, 0.0, EPS, ALU.max, ALU.add).then_inc(tail_var, 1)
                dve.wait_ge(tail_std, 1)
                link(dve.reciprocal(rstd, var))
                link(dve.tensor_scalar(tt, tt, mean, None, ALU.subtract))
                dve.tensor_scalar(tail_o[0:n, :], tt, rstd, None, ALU.mult).then_inc(tail_ready, 1)

            @block.scalar
            def _(act):
                sums_act(act)

                def squares(c, slot):
                    act.wait_ge(y_ready, c + 1)
                    if not is_first(c, 1):
                        act.wait_ge(y_squared, c)
                    pass_waits(act, "act")
                    for j in range(RJ):
                        last = act.activation(unread[:, row(j)], kept(c, slot, row(j)), ACT.Square,
                                              accum_out=row_sq[:, slot, j:j + 1])
                    last.then_inc(y_squared, 1)

                def root(c, slot):
                    act.wait_ge(var_ready, c + 1)
                    act.activation(row_var[:, slot, :], row_var[:, slot, :], ACT.Sqrt).then_inc(std_ready, 1)

                def norm(c, slot, turn):
                    act.wait_ge(coef, c + 1)
                    if not is_first(c, R):
                        act.wait_ge(out_done[slot % R], turn * 32 + 16 * (slot // R))
                    pass_waits(act, "act")
                    for j in range(NA):
                        last = act.activation(ob[:, slot % R, row(j)], kept(c, slot, row(j)), ACT.Identity,
                                              bias=row_shift[:, slot, j:j + 1], scale=row_rstd[:, slot, j:j + 1])
                    last.then_inc(normed, 1)

                def put(c, slot):
                    act.wait_ge(normed, c + 1)
                    act.wait_ge(normed_dve, c + 1)
                    pass_waits(act, "act")
                    act.dma_start(chunk(out_v, c), ob[:, slot % R, :]).then_inc(out_done[slot % R], 16)

                def body(c, slot, turn):
                    if not is_first(c, 3):
                        put(c - 3, (slot + RT - 3) % RT)
                    if not is_first(c, 2):
                        norm(c - 2, (slot + RT - 2) % RT, turn - (1 if slot < 2 else 0))
                    if not is_first(c, 1):
                        root(c - 1, (slot + RT - 1) % RT)
                    squares(c, slot)
                chunks_in_order(act, body)
                norm(C - 2, (C - 2) % RT, (C - 2) // RT)
                put(C - 3, (C - 3) % RT)
                root(C - 1, (C - 1) % RT)
                norm(C - 1, (C - 1) % RT, (C - 1) // RT)
                put(C - 2, (C - 2) % RT)
                put(C - 1, (C - 1) % RT)
                act.wait_ge(tail_var, 1)
                v = row_var[0:NTAIL, 0, 0:1]
                act.activation(v, v, ACT.Sqrt).then_inc(tail_std, 1)


_INS = ['x', 'src', 'dst', 'edge_attr_256', 'L0_gnn_w_full1', 'L0_gnn_b_full1', 'L0_gnn_w_full2', 'L0_gnn_b_full2',
        'L0_gnn_w_n1', 'L0_gnn_b_n1', 'L0_gnn_w_n2', 'L0_gnn_b_n2', 'L0_gnn_gamma_int', 'L0_gnn_beta_int',
        'L0_gnn_gamma_bn', 'L0_gnn_beta_bn']


def kernel(**inputs):
    import numpy as np
    import concourse.bacc as bacc
    from concourse.bass_utils import run_bass_kernel_spmd

    nc = bacc.Bacc("TRN2", target_bir_lowering=False, num_devices=1)
    arrays, args = {}, []
    for name in _INS:
        a = np.ascontiguousarray(inputs[name])
        arrays[f"in_{name}"] = a
        args.append(nc.dram_tensor(f"in_{name}", a.shape, mybir.dt.from_np(a.dtype), kind="ExternalInput").ap())
    shape = inputs['x'].shape
    args.append(nc.dram_tensor("out_rows", shape, F32, kind="ExternalOutput").ap())
    gnn_program(nc, *args)
    r = run_bass_kernel_spmd(nc, [arrays], core_ids=[0])
    return r.results[0]["out_rows"]
```

```python
from contextlib import ExitStack

import concourse.bass as bass
from concourse import mybir

F32 = mybir.dt.float32
F32R = mybir.dt.float32r
I32 = mybir.dt.int32
ALU = mybir.AluOpType
ACT = mybir.ActivationFunctionType

P = 128
EPS = 1e-5


def in_order(eng, body, pieces, ring):
    for first, count in pieces:
        looped = count // ring * ring if count >= 2 * ring else 0
        if looped:
            with eng.Fori(0, looped // ring) as i:
                for u in range(ring):
                    s = first + u
                    body(i * ring + s, s % ring, i + s // ring)
        for s in range(first + looped, first + count):
            body(s, s % ring, s // ring)


def gnn_program(nc, x, src, dst, edge_attr, w_full1, b_full1, w_full2, b_full2,
                w_n1, b_n1, w_n2, b_n2, gamma_int, beta_int, gamma_bn, beta_bn, out):
    N, F = x.shape
    E = edge_attr.shape[0]
    KC = 3 * F // P
    MC = F // P
    TG = 4
    GE = TG * P
    G = E // GE
    REST = E - G * GE
    TAIL = [min(P, REST - t * P) for t in range((REST + P - 1) // P)]
    assert 0 < REST and len(TAIL) == 2
    NT = (E + P - 1) // P
    DUMP = GE
    TR = (N + DUMP + 1023) // 1024 * 1024
    ZR = TR // (G + 1) // P
    assert ZR * P * (G + 1) == TR

    RJ = 5
    NJ = N // P
    C = NJ // RJ
    assert C * RJ == NJ
    NTAIL = N - NJ * P
    NMAIN = NJ * P
    RES = 30
    STREAM = C - RES

    HM = MC * GE + TG * F
    RG = 7
    assert RG % 2 == 1 and RG + 4 < G
    hm_dram = nc.dram_tensor("hm_dram", (G + 1, P, HM), F32, kind="Internal").ap()
    table = nc.dram_tensor("node_table", (TR, F), F32, kind="Internal").ap()

    w1 = [w_full1, w_n1]
    w2 = [w_full2, w_n2]
    b1 = [b_full1, b_n1]
    b2 = [b_full2, b_n2]
    H, M = 0, 1

    ctx = ExitStack()

    def sem(name):
        return ctx.enter_context(nc.semaphore(name))

    def rows_of(g):
        return [P] * TG if not (isinstance(g, int) and g == G) else TAIL

    with ctx:
        def keep(name, shape, dt=F32):
            return ctx.enter_context(nc.sbuf_tensor(name, shape, dt))

        bank = ctx.enter_context(nc.psum_tensor("bank", [P, 8, 512], F32))
        ident = keep("ident", [P, P])
        ones = keep("ones", [P, P])
        ones_r = keep("ones_r", [P, P], F32R)
        dst_col = keep("dst_col", [P, (G + 1) * TG])
        scatter_idx = keep("scatter_idx", [P, (G + 1) * TG], I32)
        earlier = keep("earlier", [P, (G + 1) * TG])
        h_scale, h_shift = keep("h_scale", [P, MC]), keep("h_shift", [P, MC])

        edge_mem = ctx.enter_context(ExitStack())
        hm_res = edge_mem.enter_context(nc.sbuf_tensor("hm_res", [P, RG, HM], F32))
        side = {}

        def groups_in_order(eng, body, pieces, ring):
            for first, count in pieces:
                side["kept"] = first < RG
                in_order(eng, body, [(first, count)], ring)

        def is_kept(g):
            return g < RG if isinstance(g, int) else side["kept"]

        def hm_of(ring, g, slot, part, rows=slice(0, P)):
            if is_kept(g):
                return hm_res[rows, bass.ds(g, 1), part].rearrange("p o n -> p (o n)")
            return ring[rows, slot, part]

        passed = {n: sem("passed_" + n) for n in ("sp", "act", "dve", "pool")}

        def pass_waits(eng, n):
            eng.sem_inc(passed[n], 1)

        def bn_coefficients(dve, mean, var, gamma, beta, scale, shift, step, var_done, std_done, scaled=None):
            n = [0]

            def link(ins):
                n[0] += 1
                ins.then_inc(step, 1)
                dve.wait_ge(step, n[0])
            dve.tensor_scalar(var, var, 0.0, EPS, ALU.max, ALU.add).then_inc(var_done, 1)
            dve.wait_ge(std_done, 1)
            link(dve.reciprocal(var, var))
            link(dve.tensor_tensor(scale, var, gamma, ALU.mult))
            if scaled:
                scaled()
            link(dve.tensor_tensor(mean, mean, scale, ALU.mult))
            link(dve.tensor_tensor(shift, beta, mean, ALU.subtract))

        def bn_std(act, var, var_done, std_done):
            act.wait_ge(var_done, 1)
            act.activation(var, var, ACT.Sqrt).then_inc(std_done, 1)

        def sb(name, shape, dt=F32):
            return edge_mem.enter_context(nc.sbuf_tensor(name, shape, dt))
        w1hl = [sb("w1_hi", [P, 2, KC, F], F32R), sb("w1_lo", [P, 2, KC, F], F32R)]
        w2hl = [sb("w2_hi", [P, 2, MC, F], F32R), sb("w2_lo", [P, 2, MC, F], F32R)]
        xT_mem = [sb("xT_hi", [P, KC * GE], F32R), sb("xT_lo", [P, KC * GE], F32R)]
        xT = [v.rearrange("p (k e) -> p k e", k=KC) for v in (xT_mem[0][:, :], xT_mem[1][:, :])]
        g_mem = sb("g_hl", [P, 4 * MC * GE], F32R)
        g_hl = [g_mem[:, v * 2 * MC * GE:(v + 1) * 2 * MC * GE].rearrange("p (b c e) -> p b c e", b=2, c=MC) for v in range(2)]
        raw = hm_res[:, RG - 2:RG, :].rearrange("p g n -> p (g n)")
        W1 = 2 * MC * 3 * F
        assert W1 + 2 * MC * F <= 2 * HM
        w1_raw = raw[:, 0:W1].rearrange("p (b c k) -> p b c k", b=2, c=MC)
        w2_raw = raw[:, W1:W1 + 2 * MC * F].rearrange("p (b c k) -> p b c k", b=2, c=MC)
        land = sb("land", [P, 2, 3, TG, F])
        g32 = sb("g32", [P, 2, GE])
        R2 = 4
        hm = sb("hm", [P, R2, HM])
        h_stats = sb("h_stats", [P, MC, (G + 1) * 6])
        h_mv = sb("h_mv", [P, MC, 2])
        b1c = sb("b1c", [P, 2, MC])
        b2c = sb("b2c", [P, MC])
        b2b = sb("b2b", [P, F])
        gamma_c, beta_c = sb("gamma_c", [P, MC]), sb("beta_c", [P, MC])
        drow = sb("drow", [P, R2, GE], I32)
        before = sb("before", [P, GE], mybir.dt.bfloat16)
        unread_eq = sb("unread_eq", [P, 10 * P], mybir.dt.bfloat16)
        zero = sb("zero", [P, F])
        idx_raw = g32[:, 0, 0:2 * P].bitcast(I32).rearrange("p (i e) -> p i e", i=2)
        idx_f = g32[:, 1, 0:2 * P].rearrange("p (i e) -> p i e", i=2)
        idx = sb("idx", [P, 2, (G + 1) * TG], I32)
        cur = sb("cur", [P, 2, 2, TG], I32)
        lane = sb("lane", [P, G + 1, TG], I32)
        lane_f = sb("lane_f", [P, (G + 1) * TG])
        dup = sb("dup", [P, (G + 1) * TG])

        c_ident, c_ones, c_mask = sem("c_ident"), sem("c_ones"), sem("c_mask")
        c_zero, c_idx = sem("c_zero"), sem("c_idx")
        idx_in, w1_in, w2_in, vec_in = sem("idx_in"), sem("w1_in"), sem("w2_in"), sem("vec_in")
        idx_float, idx_turned, idx_ready = sem("idx_float"), sem("idx_turned"), sem("idx_ready")
        w_turned, w_hi, w_lo = sem("w_turned"), sem("w_hi"), sem("w_lo")
        cur_ready = sem("cur_ready")
        land_x = [sem("land_x0"), sem("land_x1")]
        land_e = [sem("land_e0"), sem("land_e1")]
        drow_in = [sem("drow_in0"), sem("drow_in1")]
        turned, hi_ready, lo_ready = sem("turned"), sem("hi_ready"), sem("lo_ready")
        l1h_done, l1n_step = sem("l1h_done"), sem("l1n_step")
        silu_done, ghi_ready, glo_ready = sem("silu_done"), sem("ghi_ready"), sem("glo_ready")
        l2_done = [sem("l2h_done"), sem("l2n_done")]
        taken = [sem("h_taken"), sem("m_taken")]
        h_counted = sem("h_counted")
        stored = [sem("hm_stored0"), sem("hm_stored1")]
        counted, zeroed = sem("counted"), sem("zeroed")
        stats_done, bn1, idx_step = sem("stats_done"), sem("bn1"), sem("idx_step")
        bn1_var, bn1_std = sem("bn1_var"), sem("bn1_std")
        lane_made = sem("lane_made")

        bank_of = [[0, 1], [2, 3]]
        TURN, L2 = 4, 6
        units = [(1, b, k) for b in range(2) for k in range(KC)] + \
                [(2, b, k) for b in range(2) for k in range(MC)]

        def edge_rows(g, t0, rows):
            return edge_attr[bass.ds(g * GE + t0 * P, rows), :]

        def edges_sp(sp):
            sp.wait_ge(c_idx, 1)
            last = (NT - 1) * P
            for i, v in enumerate((dst, src)):
                sp.dma_start(idx_raw[0:NT - 1, i, :], v[0:last].rearrange("(t p) -> t p", p=P)).then_inc(idx_in, 16)
                sp.dma_start(idx_raw[NT - 1:NT, i, 0:E - last],
                             v[last:E].rearrange("(o p) -> o p", o=1)).then_inc(idx_in, 16)

            def load_rows(g, slot):
                rows = rows_of(g)
                if len(rows) == TG:
                    sp.dma_start(land[:, slot, 2, :, :],
                                 edge_rows(g, 0, GE).rearrange("(t p) f -> p t f", p=P)).then_inc(land_e[slot], 16)
                    sp.dma_start(drow[:, slot, :], dst[bass.ds(g * GE, GE)].rearrange("(o n) -> o n", o=1)
                                 .to_broadcast([P, GE])).then_inc(drow_in[slot], 16)
                else:
                    for t, r in enumerate(rows):
                        sp.dma_start(land[0:r, slot, 2, t, :], edge_rows(g, t, r)).then_inc(land_e[slot], 16)
                    sp.dma_start(drow[:, slot, 0:REST], dst[G * GE:E].rearrange("(o n) -> o n", o=1)
                                 .to_broadcast([P, REST])).then_inc(drow_in[slot], 16)

            for b in range(2):
                sp.dma_start(w1_raw[:, b, :, :], w1[b].rearrange("(c m) k -> m c k", m=P)).then_inc(w1_in, 16)
            for b in range(2):
                sp.dma_start(w2_raw[:, b, :, :], w2[b].rearrange("(c m) k -> m c k", m=P)).then_inc(w2_in, 16)
            sp.wait_ge(w1_in, 32)
            load_rows(0, 0)
            for b in range(2):
                sp.dma_start(b1c[:, b, :], b1[b].rearrange("(c m) -> m c", m=P), allow_slow_non_contiguous=True).then_inc(vec_in, 16)
            for to, v in ((b2c, b2[H]), (gamma_c, gamma_int), (beta_c, beta_int)):
                sp.dma_start(to[:, :], v.rearrange("(c m) -> m c", m=P), allow_slow_non_contiguous=True).then_inc(vec_in, 16)
            sp.dma_start(b2b[:, :], b2[M].rearrange("(o f) -> o f", o=1).to_broadcast([P, F])).then_inc(vec_in, 16)
            sp.wait_ge(turned, 1)
            load_rows(1, 1)
            sp.wait_ge(c_zero, 1)

            def store(g, slot):
                sp.wait_ge(taken[H], g * 2 + 2)
                pass_waits(sp, "sp")
                sp.wait_ge(taken[M], g * 2 + 2)
                pass_waits(sp, "sp")
                sp.dma_start(hm_dram[bass.ds(g, 1), :, :].rearrange("o p n -> (o p) n"),
                             hm[:, slot, :]).then_inc(stored[slot], 16)

            def body(g, slot, turn):
                sp.dma_start(table[bass.ds(g * (P * ZR), P * ZR), :].rearrange("(p j) f -> p j f", p=P),
                             zero[:, :].unsqueeze(1).to_broadcast([P, ZR, F])).then_inc(zeroed, 16)
                if not is_kept(g - 1):
                    store(g - 1, 1 - slot)
                if not (isinstance(g, int) and g + 2 > G):
                    sp.wait_ge(turned, KC * g + KC)
                    pass_waits(sp, "sp")
                    sp.wait_ge(counted, g + 1)
                    pass_waits(sp, "sp")
                    load_rows(g + 2, slot)

            groups_in_order(sp, body, [(0, 1), (1, RG - 1), (RG, 1), (RG + 1, G - 3 - RG), (G - 2, 3)], 2)
            sp.wait_ge(taken[H], 2 * G + 2)
            sp.dma_start(hm_dram[G, :, 0:MC * GE].rearrange("p (c e) -> p c e", c=MC)[:, :, 0:REST],
                         hm[:, G % 2, 0:MC * GE].rearrange("p (c e) -> p c e", c=MC)[:, :, 0:REST]).then_inc(stored[G % 2], 16)

        def finish_stores(sp):
            sp.wait_ge(taken[M], 2 * G + 1)
            for t, r in enumerate(TAIL):
                at = MC * GE + t * F
                sp.dma_start(hm_dram[G, 0:r, at:at + F], hm[0:r, G % 2, at:at + F]).then_inc(stored[G % 2], 16)
            sp.wait_ge(zeroed, 16 * (G + 1))
            sp.wait_ge(stored[G % 2], 16 * ((G - RG + 1 - (G - RG) % 2) // 2 + 1 + len(TAIL)))
            sp.wait_ge(stored[1 - G % 2], 16 * ((G - RG + (G - RG) % 2) // 2))

        def edges_pool(pool):
            pool.memset(idx_raw[:, :, :], 0).then_inc(c_idx, 1)
            pool.memset(ident[:, :], 0.0).then_inc(c_ident, 1)
            pool.wait_ge(c_ident, 1)
            pool.affine_select(out=ident[:, :], in_=ident[:, :], compare_op=ALU.not_equal, fill=1.0, base=0,
                               pattern=[[-1, P]], channel_multiplier=1).then_inc(c_ident, 1)
            pool.memset(zero[:, :], 0.0).then_inc(c_zero, 1)
            pool.memset(ones[:, :], 1.0).then_inc(c_ones, 1)
            pool.memset(ones_r[:, :].bitcast(F32), 1.0).then_inc(c_ones, 1)

            def gather(g, slot):
                n = len(rows_of(g))
                pool.tensor_copy(cur[:, slot, :, 0:n], idx[:, :, bass.ds(g * TG, n)]).then_inc(cur_ready, 1)
                pool.wait_ge(cur_ready, g + 1)
                pass_waits(pool, "pool")
                for kind in range(2):
                    for t, r in enumerate(rows_of(g)):
                        pool.indirect_dma_start(
                            out=land[0:r, slot, kind, t, :], out_offset=None, in_=x,
                            in_offset=bass.IndirectOffsetOnAxis(ap=cur[0:r, slot, kind, t:t + 1], axis=0)
                        ).then_inc(land_x[slot], 16)

            pool.wait_ge(idx_ready, 3)
            gather(0, 0)
            gather(1, 1)
            pool.memset(before[:, :], 1.0).then_inc(c_mask, 1)
            pool.wait_ge(c_mask, 1)
            pool.affine_select(out=before[:, GE - P:GE], in_=before[:, GE - P:GE], compare_op=ALU.is_gt, fill=0.0,
                               base=0, pattern=[[-1, P]], channel_multiplier=1).then_inc(c_mask, 1)
            pool.iota(lane[:, :, :], pattern=[[0, G + 1], [P, TG]], base=N, channel_multiplier=1).then_inc(lane_made, 1)

            def body(g, slot, turn):
                if not (isinstance(g, int) and g + 2 > G):
                    pool.wait_ge(turned, KC * g + KC)
                    gather(g + 2, slot)

            in_order(pool, body, [(0, 1), (1, G - 4), (G - 3, 2)], 2)

        def edges_act(act):
            for u, (layer, b, k) in enumerate(units):
                act.wait_ge(w_turned, u + 1)
                to = (w1hl if layer == 1 else w2hl)[0][:, b, k, :]
                act.activation(to, bank[:, TURN + u % 4, 0:F], ACT.Copy).then_inc(w_hi, 1)

            def round_chunk(g, k):
                n = GE if len(rows_of(g)) == TG else REST
                act.wait_ge(turned, KC * g + k + 1)
                if not (isinstance(g, int) and g == 0):
                    act.wait_ge(l1n_step, KC * g + (k + 1 - KC))
                act.activation(xT[0][:, k, 0:n], bank[:, TURN + k % 2, 0:n], ACT.Copy).then_inc(hi_ready, 1)

            def silu(g, b):
                n = GE if len(rows_of(g)) == TG else REST
                if b == H:
                    act.wait_ge(l1h_done, g + 1)
                else:
                    act.wait_ge(l1n_step, KC * g + KC)
                for c in range(MC):
                    if not (isinstance(g, int) and g == 0 and b == H):
                        act.wait_ge(glo_ready, 4 * g + 2 * b + c - 1)
                    act.activation(g32[:, c, 0:n], bank[:, bank_of[b][c], 0:n], ACT.Silu,
                                   bias=b1c[:, b, c:c + 1]).then_inc(silu_done, 1)

            def take_h(g, slot, turn):
                n = GE if len(rows_of(g)) == TG else REST
                if not is_kept(g) and not (isinstance(g, int) and g < RG + 2):
                    act.wait_ge(h_counted, g - 1)
                    act.wait_ge(stored[slot], (turn - (RG + 1 - slot) // 2) * 16)
                for c in range(MC):
                    act.wait_ge(l2_done[H], g * 2 + c + 1)
                    act.activation(hm_of(hm, g, slot, slice(c * GE, c * GE + n)), bank[:, L2 + c, 0:n], ACT.Identity,
                                   bias=b2c[:, c:c + 1]).then_inc(taken[H], 1)

            def body(g, slot, turn):
                silu(g, H)
                if not (isinstance(g, int) and g == G):
                    for k in range(KC):
                        round_chunk(g + 1, k)
                if isinstance(g, int) and g == G:
                    take_h(g, slot, turn)
                    silu(g, M)
                else:
                    silu(g, M)
                    take_h(g, slot, turn)

            for k in range(KC):
                round_chunk(0, k)
            act.wait_ge(vec_in, 16 * 6)
            groups_in_order(act, body, [(0, 1), (1, RG - 1), (RG, 2), (RG + 2, G - 3 - RG), (G - 1, 2)], 2)
            bn_std(act, h_mv[:, :, 1], bn1_var, bn1_std)

        def edges_dve(dve):
            dve.wait_ge(idx_in, 64)
            dve.tensor_copy(idx_f[:, :, :], idx_raw[:, :, :]).then_inc(idx_float, 1)
            dve.wait_ge(idx_turned, 1)
            for i in range(2):
                dve.tensor_copy(idx[:, i, 0:NT], bank[:, 0, i * P:i * P + NT]).then_inc(idx_ready, 1)
            dve.tensor_copy(dst_col[:, 0:NT], bank[:, 0, 0:NT]).then_inc(idx_ready, 1)
            dve.memset(earlier[:, :], 0.0).then_inc(idx_ready, 1)
            for u, (layer, b, k) in enumerate(units):
                dve.wait_ge(w_hi, u + 1)
                hl = w1hl if layer == 1 else w2hl
                dve.tensor_tensor(hl[1][:, b, k, :], bank[:, TURN + u % 4, 0:F],
                                  hl[0][:, b, k, :].bitcast(F32), ALU.subtract).then_inc(w_lo, 1)

            def rest_chunk(g, k):
                n = GE if len(rows_of(g)) == TG else REST
                dve.wait_ge(hi_ready, KC * g + k + 1)
                dve.tensor_tensor(xT[1][:, k, 0:n], bank[:, TURN + k % 2, 0:n],
                                  xT[0][:, k, 0:n].bitcast(F32), ALU.subtract).then_inc(lo_ready, 1)

            def split(g, b):
                n = GE if len(rows_of(g)) == TG else REST
                if not (isinstance(g, int) and g == 0):
                    dve.wait_ge(l2_done[b], g * 2)
                for c in range(MC):
                    dve.wait_ge(silu_done, 4 * g + 2 * b + c + 1)
                    dve.tensor_copy(g_hl[0][:, b, c, 0:n], g32[:, c, 0:n]).then_inc(ghi_ready, 1)
                for c in range(MC):
                    dve.wait_ge(ghi_ready, 4 * g + 2 * b + c + 1)
                    dve.tensor_tensor(g_hl[1][:, b, c, 0:n], g32[:, c, 0:n],
                                      g_hl[0][:, b, c, 0:n].bitcast(F32), ALU.subtract).then_inc(glo_ready, 1)

            def take_m(g, slot):
                rows = rows_of(g)
                if len(rows) == TG:
                    for q in range(2):
                        dve.wait_ge(l2_done[M], g * 2 + q + 1)
                        at = MC * GE + 2 * q * F
                        dve.tensor_tensor(hm_of(hm, g, slot, slice(at, at + 2 * F)).rearrange("p (t f) -> p t f", t=2),
                                          bank[:, L2 + q, :].rearrange("p (t f) -> p t f", t=2),
                                          b2b[:, :].unsqueeze(1).to_broadcast([P, 2, F]), ALU.add).then_inc(taken[M], 1)
                else:
                    dve.wait_ge(l2_done[M], g * 2 + 1)
                    for t, r in enumerate(rows):
                        at = MC * GE + t * F
                        last = dve.tensor_tensor(hm[0:r, slot, at:at + F], bank[0:r, L2, t * F:(t + 1) * F],
                                                 b2b[0:r, :], ALU.add)
                    last.then_inc(taken[M], 1)

            def count_h(g, slot):
                n = GE if len(rows_of(g)) == TG else REST
                dve.wait_ge(taken[H], g * 2 + 2)
                pass_waits(dve, "dve")
                for c in range(MC):
                    last = dve.bn_stats(h_stats[:, c, bass.ds(g * 6, 6)], hm_of(hm, g, slot, slice(c * GE, c * GE + n)))
                last.then_inc(h_counted, 1)

            def count_earlier(g, slot, turn):
                rows = rows_of(g)
                dve.wait_ge(drow_in[slot], turn * 16 + 16)
                if not (isinstance(g, int) and g == 0):
                    dve.wait_ge(counted, g)
                at = 0
                for a, r in enumerate(rows):
                    n = min((a + 1) * P, GE if len(rows) == TG else REST)
                    last = dve.scalar_tensor_tensor(
                        out=unread_eq[0:r, at:at + n], in0=drow[0:r, slot, 0:n],
                        scalar=dst_col[0:r, bass.ds(g * TG + a, 1)], in1=before[0:r, GE - P - a * P:GE - P - a * P + n],
                        op0=ALU.is_equal, op1=ALU.mult, accum_out=earlier[0:r, bass.ds(g * TG + a, 1)])
                    at += n
                last.then_inc(counted, 1)

            def body(g, slot, turn):
                split(g, H)
                if not (isinstance(g, int) and g == 0):
                    take_m(g - 1, 1 - slot)
                    count_h(g - 1, 1 - slot)
                if not (isinstance(g, int) and g == G):
                    for k in range(KC):
                        rest_chunk(g + 1, k)
                if isinstance(g, int) and g == G:
                    count_earlier(g, slot, turn)
                    count_h(g, slot)
                    receivers()
                    dve.wait_ge(h_counted, G + 1)
                    for c in range(MC):
                        last = dve.bn_aggr(h_mv[:, c, :], h_stats[:, c, :])
                    last.then_inc(stats_done, 1)
                    split(g, M)
                    dve.wait_ge(stats_done, 1)
                    bn_coefficients(dve, h_mv[:, :, 0], h_mv[:, :, 1], gamma_c[:, :], beta_c[:, :], h_scale[:, :],
                                    h_shift[:, :], bn1, bn1_var, bn1_std)
                    take_m(g, slot)
                else:
                    split(g, M)
                    count_earlier(g, slot, turn)

            def receivers():
                dve.wait_ge(lane_made, 1)
                dve.wait_ge(counted, G + 1)
                steps = [
                    lambda: dve.tensor_copy(lane_f[:, :], lane[:, :, :].rearrange("p g t -> p (g t)")),
                    lambda: dve.tensor_scalar(dup[:, :], earlier[:, :], 0.0, None, ALU.is_gt),
                    lambda: dve.tensor_tensor(lane_f[:, 0:NT], lane_f[:, 0:NT], dst_col[:, 0:NT], ALU.subtract),
                    lambda: dve.tensor_tensor(lane_f[:, 0:NT], lane_f[:, 0:NT], dup[:, 0:NT], ALU.mult),
                    lambda: dve.tensor_tensor(scatter_idx[:, 0:NT], lane_f[:, 0:NT], dst_col[:, 0:NT], ALU.add),
                ]
                for i, step in enumerate(steps):
                    step().then_inc(idx_step, 1)
                    dve.wait_ge(idx_step, i + 1)

            for k in range(KC):
                rest_chunk(0, k)
            dve.wait_ge(vec_in, 16 * 6)
            dve.wait_ge(c_mask, 2)
            dve.wait_ge(idx_ready, 4)
            groups_in_order(dve, body, [(0, 1), (1, RG - 1), (RG, 1), (RG + 1, G - 2 - RG), (G - 1, 2)], 2)

        def edges_pe(pe):
            pe.wait_ge(idx_float, 1)
            pe.wait_ge(c_ident, 2)
            for i in range(2):
                last = pe.transpose(bank[:, 0, i * P:i * P + NT], idx_f[0:NT, i, :], ident[0:NT, 0:NT])
            last.then_inc(idx_turned, 1)
            pe.wait_ge(w1_in, 32)
            for u, (layer, b, k) in enumerate(units):
                if u == units.index((2, 0, 0)):
                    pe.wait_ge(w2_in, 32)
                if u >= 4:
                    pe.wait_ge(w_lo, u - 3)
                for c in range(MC):
                    raw = (w1_raw if layer == 1 else w2_raw)[:, b, c, k * P:(k + 1) * P]
                    last = pe.transpose(bank[:, TURN + u % 4, c * P:(c + 1) * P], raw, ident[:, :])
                last.then_inc(w_turned, 1)

            def turn_chunk(g, k, slot, turn):
                rows = rows_of(g)
                n_in = 8 if len(rows) == TG else 2 * len(rows)
                if k == 0:
                    pe.wait_ge(land_x[slot], turn * 128 + 16 * n_in)
                if k == 2 * F // P:
                    pe.wait_ge(land_e[slot], turn * 16 + (16 if len(rows) == TG else 32))
                if not (isinstance(g, int) and g == 0 and k < 2):
                    pe.wait_ge(lo_ready, KC * g + k - 1)
                kind, half = divmod(k, F // P)
                for t, r in enumerate(rows):
                    last = pe.transpose(bank[:, TURN + k % 2, t * P:t * P + r],
                                        land[0:r, slot, kind, t, half * P:(half + 1) * P], ident[0:r, 0:r])
                last.then_inc(turned, 1)

            def layer1(g, b, k):
                n = GE if len(rows_of(g)) == TG else REST
                if k == 0 and not (isinstance(g, int) and g == 0):
                    pe.wait_ge(silu_done, 4 * g + (2 * b - 2))
                if b == H:
                    pe.wait_ge(lo_ready, KC * g + k + 1)
                for c in range(MC):
                    for j, (w, v) in enumerate(((0, 0), (0, 1), (1, 0))):
                        last = pe.matmul(bank[:, bank_of[b][c], 0:n], w1hl[w][:, b, k, c * P:(c + 1) * P],
                                         xT[v][:, k, 0:n], start=(k == 0 and j == 0), stop=(k == KC - 1 and j == 2))
                if b == M:
                    last.then_inc(l1n_step, 1)
                elif k == KC - 1:
                    last.then_inc(l1h_done, 1)

            def layer2_h(g):
                n = GE if len(rows_of(g)) == TG else REST
                pe.wait_ge(glo_ready, 4 * g + 2)
                for c in range(MC):
                    if not (isinstance(g, int) and g == 0):
                        pe.wait_ge(taken[M], g * 2 - 1 + c)
                    i = 0
                    for k in range(MC):
                        for w, v in ((0, 0), (0, 1), (1, 0)):
                            last = pe.matmul(bank[:, L2 + c, 0:n], w2hl[w][:, H, k, c * P:(c + 1) * P],
                                             g_hl[v][:, H, k, 0:n], start=(i == 0), stop=(i == 3 * MC - 1))
                            i += 1
                    last.then_inc(l2_done[H], 1)

            def layer2_m(g):
                rows = rows_of(g)
                pe.wait_ge(glo_ready, 4 * g + 4)
                for t, r in enumerate(rows):
                    if t % 2 == 0:
                        pe.wait_ge(taken[H], g * 2 + (1 + t // 2 if len(rows) == TG else 1))
                    i = 0
                    for k in range(MC):
                        for v, w in ((0, 0), (0, 1), (1, 0)):
                            last = pe.matmul(bank[0:r, L2 + t // 2, (t % 2) * F:(t % 2 + 1) * F],
                                             g_hl[v][:, M, k, t * P:t * P + r], w2hl[w][:, M, k, :],
                                             start=(i == 0), stop=(i == 3 * MC - 1))
                            i += 1
                    if t % 2 == 1:
                        last.then_inc(l2_done[M], 1)

            def body(g, slot, turn):
                for k in range(KC):
                    if isinstance(g, int) and g == 0 and k + 2 < KC:
                        turn_chunk(0, k + 2, 0, 0)
                    layer1(g, H, k)
                if not (isinstance(g, int) and g == 0):
                    layer2_m(g - 1)
                if isinstance(g, int) and g == G:
                    layer2_h(g)
                for k in range(KC):
                    layer1(g, M, k)
                    if not (isinstance(g, int) and g == G):
                        turn_chunk(g + 1, k, 1 - slot, turn + slot)
                if not (isinstance(g, int) and g == G):
                    layer2_h(g)

            pe.wait_ge(w_lo, len(units))
            for k in range(2):
                turn_chunk(0, k, 0, 0)
            in_order(pe, body, [(0, 1), (1, G - 2), (G - 1, 2)], 2)
            layer2_m(G)

        with ExitStack() as s2:
            def sb(name, shape, dt=F32):
                return s2.enter_context(nc.sbuf_tensor(name, shape, dt))
            hm2, drow2 = hm, drow
            msg_hl = [v[:, 0:2 * TG * F].rearrange("p (s t f) -> p s t f", s=2, t=TG) for v in xT_mem]
            same = g_mem[:, 0:2 * 10 * P].rearrange("p (s n) -> p s n", s=2)
            land_mem = land[:, :, :, :, :].rearrange("p s k t f -> p (s k t f)")
            N2 = 2 * TG * F
            assert 3 * N2 <= 2 * 3 * TG * F and N2 == 2 * MC * GE
            score = land_mem[:, 0:N2].rearrange("p (s c e) -> p s c e", s=2, c=MC)
            msg = land_mem[:, N2:2 * N2].rearrange("p (s t f) -> p s t f", s=2, t=TG)
            sums = land_mem[:, 2 * N2:3 * N2].rearrange("p (s t f) -> p s t f", s=2, t=TG)
            cur2 = sb("cur2", [P, 2, TG], I32)
            h_in, m_in, dst_in = ([sem(f"{n}_in{i}") for i in range(R2)] for n in ("h", "m", "dst"))
            scored, score_turned, msg_ready = sem("scored"), sem("score_turned"), sem("msg_ready")
            msg_hi_ready, msg_lo_ready, same_ready = sem("msg_hi_ready"), sem("msg_lo_ready"), sem("same_ready")
            combined, sums_ready, added = sem("combined"), sem("sums_ready"), sem("added")
            cur2_ready = sem("cur2_ready")
            same_at = [sum(range(b + 1)) * P for b in range(TG)]
            block = s2.enter_context(nc.Block())

            def is_first(g, n=1):
                return isinstance(g, int) and g < n

            def loads(g, slot, turn):
                return turn - (RG + R2 - 1 - slot) // R2

            def parts_of(g):
                rows = rows_of(g)
                return [(P, slice(0, TG))] if len(rows) == TG else [(r, slice(t, t + 1)) for t, r in enumerate(rows)]

            def edge_banks(first, par):
                return bank[:, first + 2 * par:first + 2 * par + 2, :].rearrange("p b (t f) -> p (b t) f", t=2)

            @block.sync
            def _(sp):
                edges_sp(sp)

                def load_h(g, slot):
                    part = slice(0, MC * GE)
                    if len(rows_of(g)) == TG:
                        sp.dma_start(hm2[:, slot, part], hm_dram[bass.ds(g, 1), :, part].rearrange("o p n -> (o p) n")).then_inc(h_in[slot], 16)
                    else:
                        sp.dma_start(hm2[:, slot, part].rearrange("p (c e) -> p c e", c=MC)[:, :, 0:REST],
                                     hm_dram[G, :, part].rearrange("p (c e) -> p c e", c=MC)[:, :, 0:REST]).then_inc(h_in[slot], 16)

                def load_m(g, slot):
                    part = slice(MC * GE, HM)
                    if len(rows_of(g)) == TG:
                        sp.dma_start(hm2[:, slot, part], hm_dram[bass.ds(g, 1), :, part].rearrange("o p n -> (o p) n")).then_inc(m_in[slot], 16)
                    else:
                        for t, r in enumerate(TAIL):
                            at = MC * GE + t * F
                            sp.dma_start(hm2[0:r, slot, at:at + F], hm_dram[G, 0:r, at:at + F]).then_inc(m_in[slot], 16)

                def load_dst(g, slot):
                    n = GE if len(rows_of(g)) == TG else REST
                    sp.dma_start(drow2[:, slot, 0:n], dst[bass.ds(g * GE, n)].rearrange("(o n) -> o n", o=1)
                                 .to_broadcast([P, n])).then_inc(dst_in[slot], 16)

                sp.wait_ge(counted, G + 1)
                for g in range(R2):
                    load_dst(g, g)
                finish_stores(sp)

                def body(g, slot, turn):
                    if not is_first(g, 1):
                        sp.wait_ge(cur2_ready, g)
                        pass_waits(sp, "sp")
                    sp.wait_ge(same_ready, g + 1)
                    pass_waits(sp, "sp")
                    load_dst(g + R2, slot)
                    if not is_kept(g + R2):
                        load_h(g + R2, slot)
                        load_m(g + R2, slot)
                groups_in_order(sp, body, [(0, 2), (2, RG - 2), (RG, G - R2 - RG), (G - R2, 1)], R2)

            SC, CS = 4, 6

            @block.vector
            def _(dve):
                edges_dve(dve)
                dve.wait_ge(taken[M], 2 * G + 1)

                def message(g, slot, turn):
                    par = slot % 2
                    if not is_first(g, 2):
                        dve.wait_ge(msg_lo_ready, g - 1)
                    dve.wait_ge(score_turned, g + 1)
                    if not is_kept(g):
                        dve.wait_ge(m_in[slot], loads(g, slot, turn) * 16 + (16 if len(rows_of(g)) == TG else 32))
                    pass_waits(dve, "dve")
                    for r, ts in parts_of(g):
                        m = hm_of(hm2, g, slot, slice(MC * GE, HM), slice(0, r)).rearrange("p (t f) -> p t f", f=F)[:, ts, :]
                        last = dve.tensor_tensor(msg[0:r, par, ts, :], edge_banks(SC, 0)[0:r, ts, :], m, ALU.mult)
                    last.then_inc(msg_ready, 1)

                def compare(g, slot, turn):
                    rows = rows_of(g)
                    dve.wait_ge(dst_in[slot], turn * 16 + 16)
                    if not is_first(g, 2):
                        dve.wait_ge(combined, g - 1)
                    for b, r in enumerate(rows):
                        n = min((b + 1) * P, GE if len(rows) == TG else REST)
                        last = dve.tensor_scalar(same[0:r, slot % 2, same_at[b]:same_at[b] + n], drow2[0:r, slot, 0:n],
                                                 dst_col[0:r, bass.ds(g * TG + b, 1)], None, ALU.is_equal)
                    last.then_inc(same_ready, 1)

                def low(g, slot):
                    par = slot % 2
                    dve.wait_ge(msg_hi_ready, g + 1)
                    for r, ts in parts_of(g):
                        last = dve.tensor_tensor(msg_hl[1][0:r, par, ts, :], msg[0:r, par, ts, :],
                                                 msg_hl[0][0:r, par, ts, :].bitcast(F32), ALU.subtract)
                    last.then_inc(msg_lo_ready, 1)

                def body(g, slot, turn):
                    low(g, slot)
                    if not (isinstance(g, int) and g == G):
                        message(g + 1, (slot + 1) % R2, turn + (slot + 1) // R2)
                        compare(g + 1, (slot + 1) % R2, turn + (slot + 1) // R2)
                message(0, 0, 0)
                compare(0, 0, 0)
                groups_in_order(dve, body, [(0, RG - 1), (RG - 1, 1), (RG, G - 2 - RG), (G - 2, 3)], R2)

            @block.scalar
            def _(act):
                edges_act(act)
                act.wait_ge(bn1, 4)
                act.wait_ge(taken[H], 2 * G + 2)

                def score_of(g, slot, turn):
                    rows = rows_of(g)
                    n = GE if len(rows) == TG else REST
                    if not is_kept(g):
                        act.wait_ge(h_in[slot], loads(g, slot, turn) * 16 + 16)
                    if not is_first(g, 2):
                        act.wait_ge(score_turned, g - 1)
                    for c in range(MC):
                        last = act.activation(score[:, slot % 2, c, 0:n], hm_of(hm2, g, slot, slice(c * GE, c * GE + n)), ACT.Sigmoid,
                                              bias=h_shift[:, c:c + 1], scale=h_scale[:, c:c + 1])
                    last.then_inc(scored, 1)

                def high(g, slot):
                    par = slot % 2
                    act.wait_ge(msg_ready, g + 1)
                    if not is_first(g, 2):
                        act.wait_ge(combined, g - 1)
                    for r, ts in parts_of(g):
                        last = act.activation(msg_hl[0][0:r, par, ts, :], msg[0:r, par, ts, :], ACT.Copy)
                    last.then_inc(msg_hi_ready, 1)

                def take_sums(g, slot):
                    par = slot % 2
                    act.wait_ge(combined, g + 1)
                    if not is_first(g, 2):
                        act.wait_ge(added, 64 * g - 64)
                    for r, ts in parts_of(g):
                        last = act.activation(sums[0:r, par, ts, :], edge_banks(0, par)[0:r, ts, :], ACT.Copy)
                    last.then_inc(sums_ready, 1)

                def body(g, slot, turn):
                    if not (isinstance(g, int) and g + 1 > G):
                        high(g + 1, slot + 1)
                    if not (isinstance(g, int) and g + 2 > G):
                        score_of(g + 2, (slot + 2) % R2, turn + (slot + 2) // R2)
                    take_sums(g, slot)
                score_of(0, 0, 0)
                score_of(1, 1, 0)
                high(0, 0)
                groups_in_order(act, body, [(0, RG - 2), (RG - 2, 2), (RG, G - 2 - RG), (G - 2, 3)], R2)

            @block.tensor
            def _(pe):
                edges_pe(pe)

                def turn_scores(g, slot):
                    par = slot % 2
                    pe.wait_ge(scored, g + 1)
                    if not is_first(g, 1):
                        pe.wait_ge(msg_ready, g)
                    for c in range(MC):
                        for t, r in enumerate(rows_of(g)):
                            last = pe.transpose(edge_banks(SC, 0)[0:r, t, c * P:(c + 1) * P],
                                                score[:, par, c, t * P:t * P + r], ident[:, :])
                    last.then_inc(score_turned, 1)

                def combine(g, slot):
                    rows, par = rows_of(g), slot % 2
                    pe.wait_ge(same_ready, g + 1)
                    pe.wait_ge(msg_lo_ready, g + 1)
                    if not is_first(g, 2):
                        pe.wait_ge(sums_ready, g - 1)
                    for a, ra in enumerate(rows):
                        for b in range(a, len(rows)):
                            for v in range(2):
                                last = pe.matmul(edge_banks(0, par)[0:ra, a, :],
                                                 same[0:rows[b], par, same_at[b] + a * P:same_at[b] + a * P + ra],
                                                 msg_hl[v][0:rows[b], par, b, :],
                                                 start=(b == a and v == 0), stop=(b == len(rows) - 1 and v == 1))
                    for b, r in enumerate(rows):
                        for v in range(2):
                            last = pe.matmul(bank[:, CS, 0:F], ones_r[0:r, :], msg_hl[v][0:r, par, b, :],
                                             start=(is_first(g, 1) and b == 0 and v == 0),
                                             stop=(isinstance(g, int) and g == G and b == len(rows) - 1 and v == 1))
                    last.then_inc(combined, 1)

                def body(g, slot, turn):
                    if not (isinstance(g, int) and g + 1 > G):
                        turn_scores(g + 1, 1 - slot)
                    combine(g, slot)
                turn_scores(0, 0)
                pe.wait_ge(taken[M], 2 * G + 1)
                in_order(pe, body, [(0, 2), (2, G - 4), (G - 2, 3)], 2)

            @block.gpsimd
            def _(pool):
                edges_pool(pool)
                pool.wait_ge(idx_step, 5)
                pool.wait_ge(zeroed, 16 * (G + 1))

                def body(g, slot, turn):
                    rows = rows_of(g)
                    pool.tensor_copy(cur2[:, slot, 0:len(rows)], scatter_idx[:, bass.ds(g * TG, len(rows))]).then_inc(cur2_ready, 1)
                    pool.wait_ge(cur2_ready, g + 1)
                    pass_waits(pool, "pool")
                    pool.wait_ge(sums_ready, g + 1)
                    pass_waits(pool, "pool")
                    if not is_first(g, 1):
                        pool.wait_ge(added, 64 * g)
                        pass_waits(pool, "pool")
                    for t, r in enumerate(rows):
                        pool.indirect_dma_start(
                            out=table, out_offset=bass.IndirectOffsetOnAxis(ap=cur2[0:r, slot, t:t + 1], axis=0),
                            in_=sums[0:r, slot, t, :], in_offset=None, compute_op=ALU.add).then_inc(added, 16)
                in_order(pool, body, [(0, 1), (1, G - 2), (G - 1, 2)], 2)
                pool.wait_ge(added, 64 * G + 16 * len(TAIL))

        edge_mem.close()
        with ExitStack() as s3:
            def sb(name, shape, dt=F32):
                return s3.enter_context(nc.sbuf_tensor(name, shape, dt))
            R = 3
            RT = 2 * R
            W = RJ * F
            assert RES % RT == 0
            res = sb("res", [P, RES, W])
            xr = sb("xr", [P, R, W])
            ob = sb("ob", [P, R, W])
            unread = sb("unread", [P, W], mybir.dt.bfloat16)
            tail_t = sb("tail_t", [P, F])
            tail_x = sb("tail_x", [P, F])
            tail_o = sb("tail_o", [P, F])
            tail_v = sb("tail_v", [P, 5])
            row_sum = sb("row_sum", [P, RT, RJ])
            row_sq = sb("row_sq", [P, RT, RJ])
            row_mean = sb("row_mean", [P, RT, RJ])
            row_var = sb("row_var", [P, RT, RJ])
            row_rstd = sb("row_rstd", [P, RT, RJ])
            row_shift = sb("row_shift", [P, RT, RJ])

            table_v = table[0:NMAIN, :].rearrange("(p c j) f -> p c (j f)", p=P, c=C)
            x_v = x[0:NMAIN, :].rearrange("(p c j) f -> p c (j f)", p=P, c=C)
            out_v = out[0:NMAIN, :].rearrange("(p c j) f -> p c (j f)", p=P, c=C)
            RD = 3
            acc2 = sb("acc2", [P, RD * F])
            shift_hl = sb("shift_hl", [64, 2 * F], F32R)
            gamma_row, beta_row = sb("gamma_row", [P, F]), sb("beta_row", [P, F])
            n_scale, n_shift = sb("n_scale", [P, F]), sb("n_shift", [P, F])
            n_mean, n_var = sb("n_mean", [P, F]), sb("n_var", [P, F])

            def chunk(v, c):
                return v[:, bass.ds(c, 1), :].rearrange("p o n -> p (o n)")

            alone = R + 2
            ahead = (RES - 1 - alone) // RT * RT
            PIECES = [(0, alone), (alone, ahead), (alone + ahead, RES + 2 - alone - ahead),
                      (RES + 2, (C - 1 - RES - 2) // RT * RT)]
            PIECES.append((sum(PIECES[-1]), C - sum(PIECES[-1])))
            stays = {}

            def chunks_in_order(eng, body):
                for first, count in PIECES:
                    stays["now"] = first < RES
                    in_order(eng, body, [(first, count)], RT)

            def in_res(c):
                return c < RES if isinstance(c, int) else stays["now"]

            def kept(c, slot, part=slice(0, W)):
                if in_res(c):
                    return res[:, bass.ds(c, 1), part].rearrange("p o n -> p (o n)")
                return res[:, RES - RT + slot, part]

            def row(j):
                return slice(j * F, (j + 1) * F)

            t_in = [sem(f"t_in{i}") for i in range(RT)]
            tail_in, sq_ready, sq_summed = sem("tail_in"), sem("sq_ready"), sem("sq_summed")
            sq_cols = sem("sq_cols")
            rows_in, tail_sq, sq_zero = sem("rows_in"), sem("tail_sq"), sem("sq_zero")
            n_step, shift_ready = sem("n_step"), sem("shift_ready")
            cols_ready, bn2, bn2_var, bn2_std = sem("cols_ready"), sem("bn2"), sem("bn2_var"), sem("bn2_std")

            SQ = 7

            def chunk_of(s):
                return s + RES if is_first(s, STREAM) else s - STREAM

            def summed(s, slot):
                if is_first(s, STREAM):
                    return res[:, RES - RT + slot, :]
                return res[:, bass.ds(s - STREAM, 1), :].rearrange("p o n -> p (o n)")

            def sums_sp(sp):
                def body(s, slot, turn):
                    if not is_first(s, RT):
                        sp.wait_ge(sq_ready, s - RT + 1)
                        pass_waits(sp, "sp")
                    sp.dma_start(summed(s, slot), chunk(table_v, chunk_of(s))).then_inc(t_in[slot], 16)
                in_order(sp, body, [(0, STREAM)], RT)
                sp.dma_start(tail_t[0:NTAIL, :], table[NMAIN:N, :]).then_inc(tail_in, 16)
                sp.dma_start(tail_x[0:NTAIL, :], x[NMAIN:N, :]).then_inc(tail_in, 16)
                for to, v in ((gamma_row, gamma_bn), (beta_row, beta_bn)):
                    sp.dma_start(to[:, :], v.rearrange("(o f) -> o f", o=1).to_broadcast([P, F])).then_inc(rows_in, 16)
                in_order(sp, body, [(STREAM, RES)], RT)

            def sums_act(act):
                def body(s, slot, turn):
                    act.wait_ge(t_in[slot], turn * 16 + 16)
                    if not is_first(s, R):
                        act.wait_ge(sq_summed, s - R + 1)
                        act.wait_ge(sq_cols, s - R + 1)
                    pass_waits(act, "act")
                    act.activation(ob[:, slot % R, :], summed(s, slot), ACT.Square).then_inc(sq_ready, 1)
                in_order(act, body, [(0, STREAM), (STREAM, RES)], RT)
                act.wait_ge(tail_in, 32)
                act.activation(tail_o[0:NTAIL, :], tail_t[0:NTAIL, :], ACT.Square).then_inc(tail_sq, 1)
                bn_std(act, n_var[:, :], bn2_var, bn2_std)

            def sums_dve(dve, scaled):
                dve.memset(shift_hl[:, :].bitcast(F32), 0.0)
                dve.memset(acc2[:, :], 0.0).then_inc(sq_zero, 1)
                dve.wait_ge(sq_zero, 1)

                def body(c, slot, turn):
                    dve.wait_ge(sq_ready, c + 1)
                    if not is_first(c, 1):
                        dve.wait_ge(sq_summed, c)
                    dve.tensor_tensor(acc2[:, :], acc2[:, :], ob[:, slot % R, 0:RD * F], ALU.add).then_inc(sq_summed, 1)
                in_order(dve, body, [(0, STREAM), (STREAM, RES)], RT)
                dve.wait_ge(rows_in, 32)
                dve.wait_ge(cols_ready, 1)
                dve.tensor_scalar(n_mean[:, :], bank[:, CS, 0:F], 1.0 / N, None, ALU.mult).then_inc(n_step, 1)
                dve.wait_ge(n_step, 1)
                dve.tensor_tensor(n_var[:, :], n_mean[:, :], n_mean[:, :], ALU.mult).then_inc(n_step, 1)
                dve.wait_ge(n_step, 2)
                dve.scalar_tensor_tensor(out=n_var[:, :], in0=bank[:, SQ, 0:F], scalar=1.0 / N, in1=n_var[:, :],
                                         op0=ALU.mult, op1=ALU.subtract).then_inc(n_step, 1)
                dve.wait_ge(n_step, 3)
                bn_coefficients(dve, n_mean[:, :], n_var[:, :], gamma_row[:, :], beta_row[:, :],
                                n_scale[:, :], n_shift[:, :], bn2, bn2_var, bn2_std, scaled)
                def twice(t, r):
                    return t[r:r + 1, :].rearrange("p (h f) -> p h f", f=F)

                def n_shift_twice(r):
                    return n_shift[r:r + 1, :].unsqueeze(1).to_broadcast([1, 2, F])
                for r in (0, 32):
                    last = dve.tensor_copy(twice(shift_hl, r), n_shift_twice(r))
                last.then_inc(n_step, 1)
                dve.wait_ge(n_step, 4)
                dve.tensor_tensor(twice(shift_hl, 32), n_shift_twice(32),
                                  twice(shift_hl, 32).bitcast(F32), ALU.subtract).then_inc(shift_ready, 1)

            def sums_pe(pe):
                def body(s, slot, turn):
                    pe.wait_ge(sq_ready, s + 1)
                    for j in range(RD, RJ):
                        last = pe.matmul(bank[:, SQ, 0:F], ones[:, :], ob[:, slot % R, row(j)],
                                         start=(is_first(s, 1) and j == RD), stop=False)
                    last.then_inc(sq_cols, 1)
                in_order(pe, body, [(0, STREAM), (STREAM, RES)], RT)
                pe.wait_ge(tail_sq, 1)
                pe.matmul(bank[:, SQ, 0:F], ones[0:NTAIL, :], tail_o[0:NTAIL, :], start=False, stop=False)
                pe.wait_ge(sq_summed, C)
                for j in range(RD):
                    last = pe.matmul(bank[:, SQ, 0:F], ones[:, :], acc2[:, row(j)], start=False, stop=(j == RD - 1))
                last.then_inc(cols_ready, 1)

            x_in = [sem(f"x_in{i}") for i in range(R)]
            t_again = [sem(f"t_again{i}") for i in range(RT)]
            t_scaled, z_ready, normed_dve = sem("t_scaled"), sem("z_ready"), sem("normed_dve")
            rest_ready = sem("rest_ready")
            y_ready, y_squared, small = sem("y_ready"), sem("y_squared"), sem("small")
            var_ready, std_ready, inverse, coef, normed = sem("var_ready"), sem("std_ready"), sem("inverse"), sem("coef"), sem("normed")
            out_done = [sem(f"out_done{i}") for i in range(R)]
            tail_ready, tail_stored, tail_step, tail_std = sem("tail_ready"), sem("tail_stored"), sem("tail_step"), sem("tail_std")
            tail_var = sem("tail_var")
            block = s3.enter_context(nc.Block())
            XB = [0, 3]
            ZP = (RJ - 1) * F
            NA = 4
            NL = 2

            @block.sync
            def _(sp):
                sums_sp(sp)

                def body(c, slot, turn):
                    if not is_first(c, R):
                        sp.wait_ge(y_ready, c - R + 1)
                        pass_waits(sp, "sp")
                    sp.dma_start(xr[:, slot % R, :], chunk(x_v, c)).then_inc(x_in[slot % R], 16)
                    if not in_res(c):
                        sp.wait_ge(normed, c - RT + 1)
                        sp.wait_ge(normed_dve, c - RT + 1)
                        pass_waits(sp, "sp")
                        sp.dma_start(kept(c, slot), chunk(table_v, c)).then_inc(t_again[slot], 16)
                chunks_in_order(sp, body)
                sp.wait_ge(tail_ready, 1)
                sp.dma_start(out[NMAIN:N, :], tail_o[0:NTAIL, :]).then_inc(tail_stored, 16)
                sp.wait_ge(tail_stored, 16)
                for i in range(R):
                    sp.wait_ge(out_done[i], 16 * ((C - i + R - 1) // R))

            @block.tensor
            def _(pe):
                sums_pe(pe)

                def body(c, slot, turn):
                    pe.wait_ge(x_in[slot % R], turn * 32 + 16 * (slot // R) + 16)
                    if not is_first(c, 2):
                        pe.wait_ge(y_ready, c - 1)
                    parts = [(XB[slot % 2] + b, b * 512, min(512, W - b * 512)) for b in range((W + 511) // 512)]
                    for b, at, n in parts:
                        pe.matmul(bank[:, b, 0:n], ident[:, :], xr[:, slot % R, at:at + n], start=True, stop=False)
                    pe.wait_ge(t_scaled, c + 1)
                    for b, at, n in parts:
                        if at + n <= ZP:
                            pe.matmul(bank[:, b, 0:n], ident[:, :], kept(c, slot, slice(at, at + n)), start=False, stop=False)
                    if is_first(c, 1):
                        pe.wait_ge(shift_ready, 1)
                    for b, at, n in parts:
                        last = pe.matmul(bank[:, b, 0:n], ones_r[0:64, :], shift_hl[:, 0:n], start=False, stop=True)
                    last.then_inc(z_ready, 1)
                chunks_in_order(pe, body)

            @block.vector
            def _(dve):
                def scale(c, slot, turn):
                    if not in_res(c):
                        dve.wait_ge(t_again[slot], (turn - RES // RT) * 16 + 16)
                    t = kept(c, slot).rearrange("p (j f) -> p j f", f=F)
                    dve.tensor_tensor(t, t, n_scale[:, :].unsqueeze(1).to_broadcast([P, RJ, F]), ALU.mult).then_inc(t_scaled, 1)

                def relu_add(c, slot, between):
                    z = bank[:, XB[slot % 2]:XB[slot % 2] + 3, :].rearrange("p b n -> p (b n)")
                    dve.wait_ge(z_ready, c + 1)
                    rest = kept(c, slot, slice(ZP, W))
                    dve.tensor_tensor(rest, rest, z[:, ZP:W], ALU.add).then_inc(rest_ready, 1)
                    for j in range(RJ):
                        if j == RJ - 1:
                            dve.wait_ge(rest_ready, c + 1)
                        last = dve.scalar_tensor_tensor(out=kept(c, slot, row(j)), in0=z[:, row(j)] if j < RJ - 1 else rest,
                                                        scalar=0.0, in1=xr[:, slot % R, row(j)],
                                                        op0=ALU.max, op1=ALU.add, accum_out=row_sum[:, slot, j:j + 1])
                        if j == RJ - 1:
                            last.then_inc(y_ready, 1)
                        elif between:
                            between[j]()

                def variance_steps(c, slot):
                    mean, var = row_mean[:, slot, :], row_var[:, slot, :]

                    def mean_of():
                        dve.wait_ge(y_ready, c + 1)
                        dve.tensor_scalar(mean, row_sum[:, slot, :], 1.0 / F, None, ALU.mult).then_inc(small, 1)

                    def mean_squared():
                        dve.wait_ge(small, 3 * c + 1)
                        dve.tensor_tensor(var, mean, mean, ALU.mult).then_inc(small, 1)

                    def variance():
                        dve.wait_ge(y_squared, c + 1)
                        dve.wait_ge(small, 3 * c + 2)
                        dve.scalar_tensor_tensor(out=var, in0=row_sq[:, slot, :], scalar=1.0 / F, in1=var,
                                                 op0=ALU.mult, op1=ALU.subtract).then_inc(small, 1)

                    def guarded():
                        dve.wait_ge(small, 3 * c + 3)
                        dve.tensor_scalar(var, var, 0.0, EPS, ALU.max, ALU.add).then_inc(var_ready, 1)
                    return [mean_of, mean_squared, variance, guarded]

                def invert(c, slot):
                    dve.wait_ge(std_ready, c + 1)
                    dve.reciprocal(row_rstd[:, slot, :], row_var[:, slot, :]).then_inc(inverse, 1)

                def shift_of(c, slot):
                    dve.wait_ge(inverse, c + 1)
                    dve.scalar_tensor_tensor(out=row_shift[:, slot, :], in0=row_mean[:, slot, :], scalar=-1.0,
                                             in1=row_rstd[:, slot, :], op0=ALU.mult, op1=ALU.mult).then_inc(coef, 1)

                def norm(c, slot, turn, first=NA):
                    dve.wait_ge(coef, c + 1)
                    if not is_first(c, R):
                        dve.wait_ge(out_done[slot % R], turn * 32 + 16 * (slot // R))
                    pass_waits(dve, "dve")
                    for j in range(first, RJ):
                        last = dve.tensor_scalar(ob[:, slot % R, row(j)], kept(c, slot, row(j)), row_rstd[:, slot, j:j + 1],
                                                 row_shift[:, slot, j:j + 1], ALU.mult, ALU.add)
                    last.then_inc(normed_dve, 1)

                def body(c, slot, turn):
                    two_back = c - 2, (slot + RT - 2) % RT
                    if not is_first(c, 2):
                        invert(*two_back)
                    if not (isinstance(c, int) and c == C - 1):
                        scale(c + 1, (slot + 1) % RT, turn + (slot + 1) // RT)
                    if not is_first(c, 2):
                        shift_of(*two_back)
                    relu_add(c, slot, [] if is_first(c, 1) else variance_steps(c - 1, (slot + RT - 1) % RT))
                    if not is_first(c, 2):
                        norm(*two_back, turn - (1 if slot < 2 else 0))
                sums_dve(dve, lambda: scale(0, 0, 0))
                n = NTAIL
                s = [0]

                def link(ins):
                    s[0] += 1
                    ins.then_inc(tail_step, 1)
                    dve.wait_ge(tail_step, s[0])
                total, squares, mean, var, rstd = (tail_v[0:n, i:i + 1] for i in range(5))
                tt = tail_t[0:n, :]
                link(dve.tensor_tensor(tt, tt, n_scale[0:n, :], ALU.mult))
                link(dve.tensor_tensor(tt, tt, n_shift[0:n, :], ALU.add))
                link(dve.tensor_tensor(tt, tt, tail_x[0:n, :], ALU.add))
                link(dve.scalar_tensor_tensor(out=tt, in0=tt, scalar=0.0, in1=tail_x[0:n, :],
                                              op0=ALU.max, op1=ALU.add, accum_out=total))
                link(dve.scalar_tensor_tensor(out=tail_o[0:n, :], in0=tt, scalar=1.0, in1=tt,
                                              op0=ALU.mult, op1=ALU.mult, accum_out=squares))
                link(dve.tensor_scalar(mean, total, 1.0 / F, None, ALU.mult))
                link(dve.tensor_tensor(var, mean, mean, ALU.mult))
                link(dve.scalar_tensor_tensor(out=var, in0=squares, scalar=1.0 / F, in1=var, op0=ALU.mult, op1=ALU.subtract))
                dve.tensor_scalar(var, var, 0.0, EPS, ALU.max, ALU.add).then_inc(tail_var, 1)
                dve.wait_ge(tail_std, 1)
                link(dve.reciprocal(rstd, var))
                link(dve.tensor_scalar(tt, tt, mean, None, ALU.subtract))
                dve.tensor_scalar(tail_o[0:n, :], tt, rstd, None, ALU.mult).then_inc(tail_ready, 1)
                chunks_in_order(dve, body)
                def finish(c):
                    invert(c, c % RT)
                    shift_of(c, c % RT)
                    norm(c, c % RT, c // RT, NA if c < C - 1 else NL)
                finish(C - 2)
                for step in variance_steps(C - 1, (C - 1) % RT):
                    step()
                finish(C - 1)

            @block.scalar
            def _(act):
                sums_act(act)

                def squares(c, slot):
                    act.wait_ge(y_ready, c + 1)
                    if not is_first(c, 1):
                        act.wait_ge(y_squared, c)
                    pass_waits(act, "act")
                    for j in range(RJ):
                        last = act.activation(unread[:, row(j)], kept(c, slot, row(j)), ACT.Square,
                                              accum_out=row_sq[:, slot, j:j + 1])
                    last.then_inc(y_squared, 1)

                def root(c, slot):
                    act.wait_ge(var_ready, c + 1)
                    act.activation(row_var[:, slot, :], row_var[:, slot, :], ACT.Sqrt).then_inc(std_ready, 1)

                def norm(c, slot, turn, rows=NA):
                    act.wait_ge(coef, c + 1)
                    if not is_first(c, R):
                        act.wait_ge(out_done[slot % R], turn * 32 + 16 * (slot // R))
                    pass_waits(act, "act")
                    for j in range(rows):
                        last = act.activation(ob[:, slot % R, row(j)], kept(c, slot, row(j)), ACT.Identity,
                                              bias=row_shift[:, slot, j:j + 1], scale=row_rstd[:, slot, j:j + 1])
                    last.then_inc(normed, 1)

                def put(c, slot):
                    act.wait_ge(normed, c + 1)
                    act.wait_ge(normed_dve, c + 1)
                    pass_waits(act, "act")
                    act.dma_start(chunk(out_v, c), ob[:, slot % R, :]).then_inc(out_done[slot % R], 16)

                def body(c, slot, turn):
                    if not is_first(c, 3):
                        put(c - 3, (slot + RT - 3) % RT)
                    if not is_first(c, 2):
                        norm(c - 2, (slot + RT - 2) % RT, turn - (1 if slot < 2 else 0))
                    if not is_first(c, 1):
                        root(c - 1, (slot + RT - 1) % RT)
                    squares(c, slot)
                act.wait_ge(tail_var, 1)
                v = tail_v[0:NTAIL, 3:4]
                act.activation(v, v, ACT.Sqrt).then_inc(tail_std, 1)
                chunks_in_order(act, body)
                norm(C - 2, (C - 2) % RT, (C - 2) // RT)
                put(C - 3, (C - 3) % RT)
                root(C - 1, (C - 1) % RT)
                norm(C - 1, (C - 1) % RT, (C - 1) // RT, NL)
                put(C - 2, (C - 2) % RT)
                put(C - 1, (C - 1) % RT)


_INS = ['x', 'src', 'dst', 'edge_attr_256', 'L0_gnn_w_full1', 'L0_gnn_b_full1', 'L0_gnn_w_full2', 'L0_gnn_b_full2',
        'L0_gnn_w_n1', 'L0_gnn_b_n1', 'L0_gnn_w_n2', 'L0_gnn_b_n2', 'L0_gnn_gamma_int', 'L0_gnn_beta_int',
        'L0_gnn_gamma_bn', 'L0_gnn_beta_bn']


def kernel(**inputs):
    import numpy as np
    import concourse.bacc as bacc
    from concourse.bass_utils import run_bass_kernel_spmd

    nc = bacc.Bacc("TRN2", target_bir_lowering=False, num_devices=1)
    arrays, args = {}, []
    for name in _INS:
        a = np.ascontiguousarray(inputs[name])
        arrays[f"in_{name}"] = a
        args.append(nc.dram_tensor(f"in_{name}", a.shape, mybir.dt.from_np(a.dtype), kind="ExternalInput").ap())
    shape = inputs['x'].shape
    args.append(nc.dram_tensor("out_rows", shape, F32, kind="ExternalOutput").ap())
    gnn_program(nc, *args)
    r = run_bass_kernel_spmd(nc, [arrays], core_ids=[0])
    return r.results[0]["out_rows"]
```
